# Optimizing a Trainium2 kernel written in Bass

```python
import numpy as np
import jax
import jax.numpy as jnp

def _softmax(x, axis=-1):
    return jax.nn.softmax(x, axis=axis)

def _gelu(x):
    return jax.nn.gelu(x, approximate=True)

def _silu(x):
    return jax.nn.silu(x)

def _sigmoid(x):
    return jax.nn.sigmoid(x)

def _layernorm(x, axis=-1, eps=1e-05):
    m = jnp.mean(x, axis=axis, keepdims=True)
    v = jnp.var(x, axis=axis, keepdims=True)
    return (x - m) / jnp.sqrt(v + eps)

def _scatter_add(tgt, idx, src, axis=0):
    return tgt.at[idx].add(src)

def _segment_sum(src, seg, n):
    return jax.ops.segment_sum(src, seg, n)
kernel_name = 'mk_cond_resid_d2_seqx_r4_db304c'

def setup_inputs(seed: int=0):
    np.random.seed(seed)
    _w = jnp.asarray

    def _rec_inputs():
        import jax
        import jax.numpy as jnp
        _rk = jax.random.key(seed)
        x = -0.0002919 + 1 * jax.random.normal(jax.random.fold_in(_rk, 1), (8, 256, 256), jnp.float32)
        _lenS = 256 - jax.random.randint(jax.random.fold_in(_rk, 7), (8,), 0, max(1, 256 // 4) + 1, jnp.int32)
        _lenS2 = 256 - jax.random.randint(jax.random.fold_in(_rk, 8), (8,), 0, max(1, 256 // 4) + 1, jnp.int32)
        cond_1024 = 0.0061147 + 1.02565 * jax.random.normal(jax.random.fold_in(_rk, 11), (8, 256), jnp.float32)
        _validS = jnp.arange(256)[None, :] < _lenS[:, None]
        _validS2 = jnp.arange(256)[None, :] < _lenS2[:, None]
        _causal = jnp.tril(jnp.ones((256, 256), dtype=bool))
        mask_Bx1x1xS_ff0 = jnp.where(jnp.ones((8, 1, 1, 256), dtype=bool), 0.0, -1000000000.0).astype(jnp.float32)
        return (x, cond_1024, mask_Bx1x1xS_ff0)
    x, cond_1024, mask_Bx1x1xS_ff0 = _rec_inputs()

    def _L0_cond_setup():
        import jax, jax.numpy as jnp
        import numpy as np
        EMBED = 256
        HEADS = 16
        HDIM = EMBED // HEADS
        MASK_OUT = -10000.0

        def _split_heads(t):
            B, T, _ = t.shape
            return t.reshape(B, T, HEADS, HDIM).transpose(0, 2, 1, 3)
        key = jax.random.key(seed)
        ks = jax.random.split(key, 12)
        B, S = (4, 1023)
        scale = 0.02
        return {'word_hidden_states': jax.random.normal(ks[0], (B, S, EMBED), jnp.float32), 'image_hidden_states': jax.random.normal(ks[1], (B, EMBED), jnp.float32), 'attention_mask': jnp.zeros((B, 1, 1, S), jnp.float32), 'c_attn_w': jax.random.normal(ks[2], (EMBED, 3 * EMBED), jnp.float32) * scale, 'c_attn_b': jnp.zeros((3 * EMBED,), jnp.float32), 'c_proj_w': jax.random.normal(ks[3], (EMBED, EMBED), jnp.float32) * scale, 'c_proj_b': jnp.zeros((EMBED,), jnp.float32), 'uk_w': jax.random.normal(ks[4], (EMBED, EMBED), jnp.float32) * scale, 'uk_b': jnp.zeros((EMBED,), jnp.float32), 'uv_w': jax.random.normal(ks[5], (EMBED, EMBED), jnp.float32) * scale, 'uv_b': jnp.zeros((EMBED,), jnp.float32)}
    _L0_cond_all = _L0_cond_setup()
    _L0_cond_in = {k: v for k, v in _L0_cond_all.items() if k in ('c_attn_w', 'c_attn_b', 'c_proj_w', 'c_proj_b', 'uk_w', 'uk_b', 'uv_w', 'uv_b')}
    del _L0_cond_all

    def _L1_cond_setup():
        import jax, jax.numpy as jnp
        import numpy as np
        LATENT = 256
        key = jax.random.key(seed)
        k1, k2, k3, k4 = jax.random.split(key, 4)
        B, T, D = (64, 128, LATENT)
        h_t = jax.random.normal(k1, (B, D), dtype=jnp.float32)
        z = jax.random.normal(k2, (B, T, D), dtype=jnp.float32)
        bound = 1.0 / np.sqrt(2 * D)
        W = jax.random.uniform(k3, (D, 2 * D), minval=-bound, maxval=bound, dtype=jnp.float32)
        b = jax.random.uniform(k4, (D,), minval=-bound, maxval=bound, dtype=jnp.float32)
        alpha = jnp.full((D,), 0.1, dtype=jnp.float32)
        return {'h_t': h_t, 'z': z, 'W': W, 'b': b, 'alpha': alpha}
    _L1_cond_all = _L1_cond_setup()
    _L1_cond_in = {k: v for k, v in _L1_cond_all.items() if k in ('W', 'b', 'alpha')}
    del _L1_cond_all
    return {'x': x, 'cond_1024': cond_1024, 'mask_Bx1x1xS_ff0': mask_Bx1x1xS_ff0, 'L0_cond_c_attn_w': _L0_cond_in['c_attn_w'], 'L0_cond_c_attn_b': _L0_cond_in['c_attn_b'], 'L0_cond_c_proj_w': _L0_cond_in['c_proj_w'], 'L0_cond_c_proj_b': _L0_cond_in['c_proj_b'], 'L0_cond_uk_w': _L0_cond_in['uk_w'], 'L0_cond_uk_b': _L0_cond_in['uk_b'], 'L0_cond_uv_w': _L0_cond_in['uv_w'], 'L0_cond_uv_b': _L0_cond_in['uv_b'], 'L1_cond_W': _L1_cond_in['W'], 'L1_cond_b': _L1_cond_in['b'], 'L1_cond_alpha': _L1_cond_in['alpha']}

def reference(x, cond_1024, mask_Bx1x1xS_ff0, L0_cond_c_attn_w, L0_cond_c_attn_b, L0_cond_c_proj_w, L0_cond_c_proj_b, L0_cond_uk_w, L0_cond_uk_b, L0_cond_uv_w, L0_cond_uv_b, L1_cond_W, L1_cond_b, L1_cond_alpha):
    import jax
    import jax.numpy as jnp

    def _L0_cond_ref(word_hidden_states, image_hidden_states, attention_mask, c_attn_w, c_attn_b, c_proj_w, c_proj_b, uk_w, uk_b, uv_w, uv_b):
        import jax, jax.numpy as jnp
        import numpy as np
        EMBED = 256
        HEADS = 16
        HDIM = EMBED // HEADS
        MASK_OUT = -10000.0

        def _split_heads(t):
            B, T, _ = t.shape
            return t.reshape(B, T, HEADS, HDIM).transpose(0, 2, 1, 3)
        B, S, _ = word_hidden_states.shape
        qkv = word_hidden_states @ c_attn_w + c_attn_b
        q_word, k_word, v_word = jnp.split(qkv, 3, axis=-1)
        img = image_hidden_states[:, None, :]
        k_img = img @ uk_w.T + uk_b
        v_img = img @ uv_w.T + uv_b
        k = jnp.concatenate([k_img, k_word], axis=1)
        v = jnp.concatenate([v_img, v_word], axis=1)
        q = _split_heads(q_word)
        k = _split_heads(k)
        v = _split_heads(v)
        scores = jnp.einsum('bhqd,bhkd->bhqk', q, k) / jnp.sqrt(jnp.float32(HDIM))
        qi = jnp.arange(S)[:, None]
        kj = jnp.arange(S + 1)[None, :]
        causal = kj <= qi + 1
        scores = jnp.where(causal[None, None], scores, jnp.float32(MASK_OUT))
        zero_col = jnp.zeros(attention_mask.shape[:-1] + (1,), attention_mask.dtype)
        mask = jnp.concatenate([zero_col, attention_mask], axis=-1)
        scores = scores + mask
        attn = jax.nn.softmax(scores, axis=-1)
        out = jnp.einsum('bhqk,bhkd->bhqd', attn, v)
        out = out.transpose(0, 2, 1, 3).reshape(B, S, EMBED)
        out = out @ c_proj_w + c_proj_b
        return out

    def _L1_cond_ref(h_t, z, W, b, alpha):
        import jax, jax.numpy as jnp
        import numpy as np
        LATENT = 256
        D = h_t.shape[-1]
        Wh = W[:, :D]
        Wz = W[:, D:]
        leak = 1.0 - alpha

        def step(h, z_t):
            gate = jax.nn.sigmoid(h @ Wh.T + z_t @ Wz.T + b)
            h_new = jnp.tanh(h * leak + gate * z_t)
            return (h_new, h_new)
        _, hs = jax.lax.scan(step, h_t, jnp.swapaxes(z, 0, 1))
        return jnp.swapaxes(hs, 0, 1)
    x = x + _L0_cond_ref(x, cond_1024, mask_Bx1x1xS_ff0, L0_cond_c_attn_w, L0_cond_c_attn_b, L0_cond_c_proj_w, L0_cond_c_proj_b, L0_cond_uk_w, L0_cond_uk_b, L0_cond_uv_w, L0_cond_uv_b)
    x = x + _L1_cond_ref(cond_1024, x, L1_cond_W, L1_cond_b, L1_cond_alpha)
    return x

_drawn_inputs = setup_inputs


def setup_inputs(seed=0):
    import zlib

    import numpy as np

    out = dict(_drawn_inputs(seed))
    spreads = {'L0_cond_c_attn_b': (0.0, 0.1),
     'L0_cond_c_proj_b': (0.0, 0.1),
     'L0_cond_uk_b': (0.0, 0.8),
     'L0_cond_uv_b': (0.0, 0.8),
     'L1_cond_alpha': (0.10000000149011612, 0.6)}
    factors = {'L0_cond_c_attn_w': 2.855, 'L0_cond_uk_w': 8.0, 'L0_cond_uv_w': 8.0, 'L1_cond_b': 8.0}
    for name, (base, spread) in spreads.items():
        noise = np.random.default_rng([zlib.crc32(name.encode()), seed]).standard_normal(out[name].shape)
        drawn = base * np.exp(spread * noise) if base else spread * noise
        out[name] = jnp.asarray(drawn.astype(out[name].dtype))
    for name, factor in factors.items():
        out[name] = (out[name] * factor).astype(out[name].dtype)
    return out
```

```python
import concourse.bass as bass
from concourse import mybir
from contextlib import ExitStack

F32 = mybir.dt.float32
BF16 = mybir.dt.bfloat16
F16 = mybir.dt.float16
ALU = mybir.AluOpType
ACT = mybir.ActivationFunctionType
AX_X = mybir.AxisListType.X

P = 128
HIDDEN_SCORE = -30000.0

PAIRS = [(0, 0), (0, 1), (1, 0), (1, 1), (0, 2), (2, 0)]


def build(nc, x, cond, mask, attn_w, attn_b, proj_w, proj_b, uk_w, uk_b, uv_w, uv_b, rec_w, rec_b, alpha, out):
    B, S, E = x.shape
    H, D = 16, 16
    EC = E // P
    TB = S // P
    G = H // 4
    HALF = B // 2
    NQ = HALF * P
    SLOTS = len(PAIRS) * D
    MASK0, SHIFT0, ROWS = SLOTS, SLOTS + 3, SLOTS + 6
    STEP = EC * B
    GS = 16
    NG = S // GS

    ctx = ExitStack()
    with ctx:
        def sb(name, shape, dt=F32):
            return ctx.enter_context(nc.sbuf_tensor(name, shape, dt))

        def sem(name):
            return ctx.enter_context(nc.semaphore(name))

        def dram(name, shape, dt):
            return nc.dram_tensor(name, shape, dt, kind="Internal").ap()

        xin = sb("xin", [P, TB, B, E])
        region = sb("region", [P, 10 * NQ])

        def view(first, count, pattern=None, **sizes):
            v = region[:, first * NQ:(first + count) * NQ]
            return v.rearrange(pattern, **sizes) if pattern else v

        full = view(0, 2, "p (a n) -> p a n", a=2)
        rest = view(2, 1)
        w_attn = view(3, 3, "p (c e) -> p c e", c=EC)
        w_uk = view(6, 1, "p (c e) -> p c e", c=EC)
        w_uv = view(7, 1, "p (c e) -> p c e", c=EC)
        ukT = view(8, 1, "p (c e) -> p c e", c=EC)
        uvT = view(9, 1, "p (c e) -> p c e", c=EC)
        prob = view(0, 4, "p (a c n) -> p a c n", a=2, c=2)
        att = view(4, 4, "p (g b q) -> p g b q", g=G, b=HALF)
        att_raw = view(8, 1)
        att_inv = view(9, 1)
        y_out = view(0, 2, "p (a b e) -> p a b e", a=2, b=2)
        w_proj = sb("w_proj", [P, G, E])
        w_rec = sb("w_rec", [P, EC, 2 * E])
        cond_in = sb("cond_in", [B, E])
        bias_rows = sb("bias_rows", [5 * EC, P])
        bias_cols = sb("bias_cols", [P, 5 * EC])
        b_qk, b_uk = bias_cols[:, 0:2 * EC], bias_cols[:, 2 * EC:3 * EC]
        b_proj, alpha_in = bias_cols[:, 3 * EC:4 * EC], bias_cols[:, 4 * EC:5 * EC]
        b_v = sb("b_v", [P, E])
        b_uv = sb("b_uv", [H, E])
        b_rec = sb("b_rec", [1, E])
        ident = sb("ident", [P, P])
        ident_b = sb("ident_b", [P, P], BF16)
        causal_qk = sb("causal_qk", [P, P], BF16)
        causal_kq = sb("causal_kq", [P, P], BF16)
        ones_row = sb("ones_row", [1, P])
        sel_den = sb("sel_den", [P, P])
        own_head = sb("own_head", [H, E])

        xT = sb("xT", [P, EC, TB, B, P])
        zT = xT
        condT = sb("condT", [P, EC, B])
        parts = sb("parts", [P, 2, 3, NQ], BF16)
        parts_img = sb("parts_img", [P, 3, EC, B], BF16)
        img_full = sb("img_full", [P, EC, B])
        img_rest = sb("img_rest", [P, EC, B])
        mask_parts = sb("mask_parts", [B, 3, S], BF16)
        Kst = sb("Kst", [P, TB, H, B * P], BF16)
        Qst = sb("Qst", [P, H, B * P], BF16)
        Kimg = sb("Kimg", [SLOTS, H, B], BF16)
        Kdiag = sb("Kdiag", [P, B, H, H], BF16)
        V = sb("V", [P, TB, B, H, D + 1])
        Vimg = xin[0:H].rearrange("h t b e -> h (t b e)").rearrange("h (b g c) -> h b g c", b=B, g=G)
        row_max = sb("row_max", [P, B * H])
        shift = sb("shift", [P, P])
        shift_rest = row_max
        shift_parts = sb("shift_parts", [P, 3, P], BF16)
        prob_img = sb("prob_img", [H, P])

        whT = sb("whT", [P, EC, E])
        wzT = sb("wzT", [P, EC, E])
        wh_rest = sb("wh_rest", [P, EC * E])
        mask_in, mask_rest = wh_rest[0:B, 0:S], wh_rest[0:B, S:2 * S]
        wh_parts = sb("wh_parts", [P, 3, EC, E], BF16)
        leak = sb("leak", [P, EC])
        zq = w_rec[:].rearrange("p c e -> p (c e)").rearrange("p (a t c i) -> p a t c i", a=2, t=GS, i=2)
        Hf = sb("Hf", [P, 2 * GS, STEP])
        ones_rows = Hf[0:3, 0:GS].rearrange("p t c -> p (t c)").bitcast(BF16)
        H1 = sb("H1", [P, 2, STEP], F16)
        H2 = sb("H2", [P, 2, STEP], F16)
        gate = sb("gate", [P, 2, STEP, 2])
        arg = sb("arg", [P, 2, STEP, 2])

        pG = [ctx.enter_context(nc.psum_tensor(f"pG{i}", [P, 32, STEP], F32)) for i in range(2)]
        pA = [ctx.enter_context(nc.psum_tensor(f"pA{i}", [P, 2, 512], F32)) for i in range(2)]
        pV = ctx.enter_context(nc.psum_tensor("pV", [P, 512], F32))
        pX = ctx.enter_context(nc.psum_tensor("pX", [P, 512], F32))

        scr = {"k": dram("scr_k", [3, E, TB, B * P], BF16), "q": dram("scr_q", [3, E, TB, B * P], BF16)}
        scr_img = dram("scr_img", [3, E, B], BF16)
        scr_mask = dram("scr_mask", [3, TB, B, P], BF16)

        names = """in_x0 in_x1 in_cond in_uk in_attn in_small in_uv in_rec in_mask in_proj consts
            tile_full act_tiles dve_tiles kq_hi kq_mid kq_rest kq_low kq_stored0 kq_stored1 img_hi img_rest_s img_mid img_low img_stored
            mask_p mask_stored ones_k ones_q stack_k0 stack_k1 stack_img stack_mask stack_q0 stack_q1 kdiag_ready v_rows vimg_ready
            max_full max_read maxT_full shift_step shift_sent
            img_scores img_prob score_full prob_ready pv_full att_copied den_full att_step proj_full z_ready
            wh_split leak_ready h0_ready zq_ready y_ready seeded gate_sum gate_ready h_hi h_full h_low q_ready arg_ready
            yt_full yt_copied out_sent0 out_sent1 b_scaled bias_ready prob_used""".split()
        s = {n: sem(n) for n in names}

        block = ctx.enter_context(nc.Block())

        def token_tiles(tb):
            return ([("k", (tb, m, hf), "act") for m in range(EC) for hf in range(2)]
                    + ([("kimg", (), "act")] if tb == 0 else [])
                    + [("q", (tb, m, hf), "act") for m in range(EC) for hf in range(2)]
                    + [("v", (tb, b), "dve") for b in range(0, B, 2)])

        def x_tiles(tb):
            return [("x", (tb, k, hf), "act") for k in range(EC) for hf in range(2)]

        TILES = (x_tiles(0) + [("cond", (), "act"), ("uk", (), "act")] + token_tiles(0) + x_tiles(1)
                 + [("uv", (), "act")] + [("vimg", b, "dve") for b in range(0, B, 2)]
                 + [("wh", (), "act"), ("wz", (), "act")] + token_tiles(1))
        BANKS = 4

        def bank(n):
            return pA[n % BANKS // 2][:, n % 2, :]

        def tiles_done(engine, n):
            return sum(t[2] == engine for t in TILES[:n + 1])

        def wait_tile_empty(eng, n):
            who = TILES[n][2]
            eng.wait_ge(s["act_tiles" if who == "act" else "dve_tiles"], tiles_done(who, n))

        def tile_at(kind, where=None):
            return next(n for n, t in enumerate(TILES) if t[0] == kind and (where is None or t[1] == where))

        SPLITS = [t for t in TILES if t[0] in "kq"]

        def split_at(kind, tb, last=True):
            return max(n for n, t in enumerate(SPLITS) if t[0] == kind and t[1][0] == tb)

        def wait_stored(eng, n):
            eng.wait_ge(s[f"kq_stored{n % 2}"], 16 * (n // 2 + 1))

        HEADS_OF_TILE = [4, 2]
        max_tiles = [(qb, b, h) for qb in range(TB) for b in range(B) for h in range(0, H, HEADS_OF_TILE[qb])]

        def max_region(n, j, qb):
            cols = 1 + P * (qb + 1)
            per = HEADS_OF_TILE[qb] // 2
            return pA[n % 2][:, j // per, (j % per) * cols:(j % per + 1) * cols]

        def max_done(qb):
            return sum(t[0] <= qb for t in max_tiles)

        units = [(qb, b, g) for qb in range(TB) for b in range(B) for g in range(G)]

        CONSTS = 14 + 8

        @block.sync
        def _(sp):
            sp.dma_start(xin[:, 0], x[:, 0:P, :].rearrange("b p e -> p b e")).then_inc(s["in_x0"], 16)
            sp.dma_start(cond_in[:], cond).then_inc(s["in_cond"], 16)
            sp.dma_start(w_uk[:], uk_w.rearrange("(c p) e -> p c e", p=P)).then_inc(s["in_uk"], 16)
            sp.dma_start(w_attn[:], attn_w.rearrange("(c p) e -> p c e", p=P)).then_inc(s["in_attn"], 16)
            for row, vec in ((0, attn_b[0:2 * E]), (2 * EC, uk_b), (3 * EC, proj_b), (4 * EC, alpha)):
                rows = vec.rearrange("(m p) -> m p", p=P)
                sp.dma_start(bias_rows[row:row + rows.shape[0]], rows).then_inc(s["in_small"], 16)
            sp.dma_start(b_v[:], attn_b[2 * E:3 * E].rearrange("(a e) -> a e", a=1).to_broadcast([P, E])
                         ).then_inc(s["in_small"], 16)
            sp.dma_start(b_uv[:], uv_b.rearrange("(a e) -> a e", a=1).to_broadcast([H, E])).then_inc(s["in_small"], 16)
            sp.dma_start(b_rec[:], rec_b.rearrange("(a e) -> a e", a=1)).then_inc(s["in_small"], 16)
            sp.dma_start(mask_in[:], mask.rearrange("b i j k -> (b i j) k")).then_inc(s["in_mask"], 16)
            sp.dma_start(w_uv[:], uv_w.rearrange("(c p) e -> p c e", p=P)).then_inc(s["in_uv"], 16)
            sp.dma_start(w_rec[:], rec_w.rearrange("(c p) e -> p c e", p=P)).then_inc(s["in_rec"], 16)
            sp.dma_start(xin[:, 1], x[:, P:S, :].rearrange("b p e -> p b e")).then_inc(s["in_x1"], 16)

            sp.wait_ge(s["consts"], CONSTS)
            ones = ones_rows[:, None, :]
            ones_n = 2 * GS * STEP
            sp.dma_start(Kst[SHIFT0:SHIFT0 + 3].rearrange("i t h (c n) -> i (t h c) n", n=ones_n),
                         ones.to_broadcast([3, TB * H * B * P // ones_n, ones_n])
                         ).then_inc(s["ones_k"], 16)
            sp.dma_start(Qst[MASK0:MASK0 + 3].rearrange("i h (c n) -> i (h c) n", n=ones_n),
                         ones.to_broadcast([3, H * B * P // ones_n, ones_n])).then_inc(s["ones_q"], 16)

            for j in range(4):
                sp.dma_start(w_proj[32 * j:32 * j + D], proj_w.rearrange("(g j d) n -> j d g n", g=G, j=4)[j]
                             ).then_inc(s["in_proj"], 16)

            def store_split(n):
                kind, (tb, m, hf), _ = SPLITS[n]
                sp.wait_ge(s["kq_hi"], 2 * (n + 1))
                sp.wait_ge(s["kq_mid"], n + 1)
                sp.wait_ge(s["kq_low"], n + 1)
                sp.dma_start(scr[kind][:, m * P:(m + 1) * P, tb, hf * NQ:(hf + 1) * NQ].rearrange("i p n -> p i n"),
                             parts[:, n % 2]).then_inc(s[f"kq_stored{n % 2}"], 16)

            def stack(kind, tb):
                dst = Kst[:, tb] if kind == "k" else Qst
                wait_stored(sp, split_at(kind, tb))
                wait_stored(sp, split_at(kind, tb) - 1)
                for i, (pq, pk) in enumerate(PAIRS):
                    src = scr[kind][pk if kind == "k" else pq, :, tb, :].rearrange("(h d) n -> d h n", d=D)
                    sp.dma_start(dst[i * D:(i + 1) * D], src).then_inc(s[f"stack_{kind}{tb}"], 16)

            for n in range(4):
                store_split(n)
            stack("k", 0)
            sp.wait_ge(s["img_low"], 1)
            sp.dma_start(scr_img.rearrange("i (m p) b -> p i m b", p=P), parts_img[:]).then_inc(s["img_stored"], 16)
            sp.wait_ge(s["img_stored"], 16)
            for i, (pq, pk) in enumerate(PAIRS):
                sp.dma_start(Kimg[i * D:(i + 1) * D], scr_img[pk].rearrange("(h d) b -> d h b", d=D)
                             ).then_inc(s["stack_img"], 16)
            sp.wait_ge(s["mask_p"], 5)
            for i in range(3):
                sp.dma_start(scr_mask[i].rearrange("t b q -> b t q"),
                             mask_parts[:, i, :].rearrange("b (t q) -> b t q", t=TB)).then_inc(s["mask_stored"], 16)
            for n in range(4, 8):
                store_split(n)
            stack("q", 0)
            sp.wait_ge(s["mask_stored"], 48)
            for tb in range(TB):
                for h in range(H):
                    sp.dma_start(Kst[MASK0:MASK0 + 3, tb, h, :],
                                 scr_mask[:, tb].rearrange("i b q -> i (b q)")).then_inc(s["stack_mask"], 16)
            for n in range(8, 12):
                store_split(n)
            stack("k", 1)
            for n in range(12, 16):
                store_split(n)

            def send_shift(qb):
                sp.wait_ge(s["shift_step"], 5 * (qb + 1))
                for i in range(3):
                    sp.dma_start(Qst[SHIFT0 + i:SHIFT0 + i + 1].rearrange("o h (b q) -> o (h b) q", b=B),
                                 shift_parts[:, i, :]).then_inc(s["shift_sent"], 16)

            send_shift(0)
            sp.wait_ge(s["score_full"], B * G)
            stack("q", 1)
            send_shift(1)

            for n in range(TB * B // 2):
                tb, b = n // (B // 2), 2 * (n % (B // 2))
                sp.wait_ge(s["yt_copied"], n + 1)
                sp.dma_start(out[b:b + 2, tb * P:(tb + 1) * P, :].rearrange("b p e -> p b e"),
                             y_out[:, n % 2]).then_inc(s[f"out_sent{n % 2}"], 16)
            for half in range(2):
                sp.wait_ge(s[f"out_sent{half}"], 16 * (TB * B // 4))

        @block.gpsimd
        def _(pool):
            def step(ins):
                ins.then_inc(s["consts"], 1)
                pool.wait_ge(s["consts"], n + 1)
                return 1
            n = 0
            n += step(pool.memset(w_proj[:], 0.0))
            n += step(pool.memset(ident[:], 0.0))
            n += step(pool.memset(ident_b[:], 0.0))
            n += step(pool.memset(causal_qk[:], 0.0))
            n += step(pool.memset(causal_kq[:], 0.0))
            n += step(pool.memset(sel_den[:], 0.0))
            n += step(pool.memset(own_head[:], 1.0))
            n += step(pool.memset(ones_row[:], 1.0))
            n += step(pool.memset(V[:], 1.0))
            n += step(pool.memset(ones_rows, 1.0))
            n += step(pool.memset(Kdiag[:], 0.0))
            n += step(pool.memset(gate[:], 0.0))
            n += step(pool.memset(H1[:], 0.0))
            n += step(pool.memset(H2[:], 0.0))
            for m in (ident, ident_b):
                n += step(pool.affine_select(out=m[:], in_=m[:], compare_op=ALU.not_equal, fill=1.0, base=0,
                                             pattern=[[-1, P]], channel_multiplier=1))
            n += step(pool.affine_select(out=causal_qk[:], in_=causal_qk[:], compare_op=ALU.is_ge, fill=HIDDEN_SCORE, base=0,
                               pattern=[[-1, P]], channel_multiplier=1))
            n += step(pool.affine_select(out=causal_kq[:], in_=causal_kq[:], compare_op=ALU.is_ge, fill=HIDDEN_SCORE, base=0,
                               pattern=[[1, P]], channel_multiplier=-1))
            sel = sel_den[:].rearrange("p (j c) -> p j c", j=4)
            n += step(pool.affine_select(out=sel, in_=sel, compare_op=ALU.not_equal, fill=1.0, base=-D,
                               pattern=[[-32, 4], [0, 32]], channel_multiplier=1))
            own = own_head[:].rearrange("p (h d) -> p h d", h=H)
            n += step(pool.affine_select(out=own, in_=own, compare_op=ALU.is_equal, fill=0.0, base=0,
                               pattern=[[-1, H], [0, D]], channel_multiplier=1))
            diag = Kdiag[SLOTS:P].rearrange("p b h c -> p b (h c)")[:, :, 0:H * H:H + 1]
            n += step(pool.memset(diag, 1.0))
            n += step(pool.affine_select(out=diag, in_=diag, compare_op=ALU.is_ge, fill=0.0, base=-(SHIFT0 - SLOTS),
                               pattern=[[0, B], [0, H]], channel_multiplier=1))

            for i in range(len(SPLITS)):
                pool.wait_ge(s["kq_hi"], 2 * (i + 1))
                if i >= 2:
                    wait_stored(pool, i - 2)
                pool.tensor_tensor(parts[:, i % 2, 1], full[:, i % 2], parts[:, i % 2, 0], ALU.subtract
                                   ).then_inc(s["kq_mid"], 1)

            def z_of(g):
                return zT[:, :, :, :, :].rearrange("p k t b q -> p k (t b) q")

            def halve(g):
                tb, q0 = (g * GS) // P, (g * GS) % P
                if g >= 2:
                    pool.wait_ge(s["arg_ready"], GS * (g - 1))
                    pool.wait_ge(s["seeded"], 6 * (g - 1))
                pool.wait_ge(s["z_ready"], 2 * EC * (tb + 1))
                for k in range(EC):
                    src = zT[:, k, tb, :, q0:q0 + GS].rearrange("p b q -> p q b")
                    pool.tensor_scalar(zq[:, g % 2, :, k * B:(k + 1) * B, 0], src, 0.5, None, ALU.mult
                                       ).then_inc(s["zq_ready"], 1)

            def add_z(g):
                tb, q0 = (g * GS) // P, (g * GS) % P
                pool.wait_ge(s["h_full"], GS * (g + 1))
                pool.wait_ge(s["zq_ready"], EC * (g + 1))
                for k in range(EC):
                    z = zT[:, k, tb, :, q0:q0 + GS].rearrange("p b q -> p q b")
                    h = Hf[:, (g % 2) * GS:(g % 2 + 1) * GS, k * B:(k + 1) * B]
                    pool.tensor_tensor(z, z, h, ALU.add).then_inc(s["y_ready"], 1)

            halve(0)
            halve(1)
            for g in range(NG):
                add_z(g)
                if g + 2 < NG:
                    halve(g + 2)

        

        @block.tensor
        def _(pe):
            pe.wait_ge(s["consts"], CONSTS)
            seen = set()

            def wait_input(name, value=16):
                if name not in seen:
                    seen.add(name)
                    pe.wait_ge(s[name], value)

            for n, (kind, where, who) in enumerate(TILES):
                if n >= BANKS:
                    wait_tile_empty(pe, n - BANKS)
                ps = bank(n)
                if kind == "x":
                    tb, k, hf = where
                    wait_input(f"in_x{tb}")
                    for i in range(HALF):
                        last = pe.transpose(ps[:, i * P:(i + 1) * P], xin[:, tb, hf * HALF + i, k * P:(k + 1) * P],
                                            ident[:])
                elif kind == "cond":
                    wait_input("in_cond")
                    wait_input("in_small", 16 * 7)
                    pe.transpose(ps[:, STEP:STEP + 5 * EC], bias_rows[:], ident[0:5 * EC, 0:5 * EC])
                    for k in range(EC):
                        last = pe.transpose(ps[:, k * B:(k + 1) * B], cond_in[:, k * P:(k + 1) * P], ident[0:B, 0:B])
                elif kind in ("uk", "uv"):
                    wait_input("in_" + kind)
                    w = w_uk if kind == "uk" else w_uv
                    for k in range(EC):
                        for m in range(EC):
                            last = pe.transpose(ps[:, k * E + m * P:k * E + (m + 1) * P], w[:, m, k * P:(k + 1) * P],
                                                ident[:])
                elif kind in ("wh", "wz"):
                    wait_input("in_rec")
                    o = 0 if kind == "wh" else E
                    for k in range(EC):
                        for m in range(EC):
                            last = pe.transpose(ps[:, k * E + m * P:k * E + (m + 1) * P],
                                                w_rec[:, m, o + k * P:o + (k + 1) * P], ident[:])
                elif kind in ("k", "q"):
                    tb, m, hf = where
                    wait_input("in_attn")
                    wait_tile_empty(pe, tile_at("x", (tb, EC - 1, 1)))
                    o = (0 if kind == "q" else E) + m * P
                    for k in range(EC):
                        last = pe.matmul(ps, w_attn[:, k, o:o + P],
                                         xT[:, k, tb, hf * HALF:(hf + 1) * HALF, :].rearrange("p b q -> p (b q)"),
                                         start=(k == 0), stop=(k == EC - 1))
                elif kind == "kimg":
                    wait_tile_empty(pe, tile_at("uk"))
                    for m in range(EC):
                        for k in range(EC):
                            last = pe.matmul(ps[:, m * B:(m + 1) * B], ukT[:, k, m * P:(m + 1) * P], condT[:, k, :],
                                             start=(k == 0), stop=(k == EC - 1), skip_group_check=True)
                elif kind == "v":
                    tb, b0 = where
                    wait_input("in_attn")
                    wait_tile_empty(pe, tile_at("x", (tb, EC - 1, 1)))
                    for i in range(2):
                        for k in range(EC):
                            last = pe.matmul(ps[:, i * E:(i + 1) * E], xT[:, k, tb, b0 + i, :],
                                             w_attn[:, k, 2 * E:3 * E], start=(k == 0), stop=(k == EC - 1),
                                             skip_group_check=True)
                elif kind == "vimg":
                    wait_tile_empty(pe, tile_at("uv"))
                    for i in range(2):
                        for k in range(EC):
                            last = pe.matmul(ps[0:H, i * E:(i + 1) * E],
                                             condT[:, k, where + i:where + i + 1].to_broadcast([P, H]), uvT[:, k, :],
                                             start=(k == 0), stop=(k == EC - 1), skip_group_check=True)
                last.then_inc(s["tile_full"], 1)

            def maxima(qb):
                for n, (q, b, h0) in enumerate(max_tiles):
                    if q != qb:
                        continue
                    if n >= 2:
                        pe.wait_ge(s["max_read"], n - 1)
                    for j in range(HEADS_OF_TILE[qb]):
                        h = h0 + j
                        region = max_region(n, j, qb)
                        lhs = Qst[:, h, b * P:(b + 1) * P]
                        pe.matmul(region[:, 0:1], lhs[0:SLOTS], Kimg[:, h, b:b + 1], start=True, stop=True,
                                  skip_group_check=True)
                        for c in range(qb + 1):
                            cols = region[:, 1 + c * P:1 + (c + 1) * P]
                            last = pe.matmul(cols, lhs[0:SHIFT0], Kst[0:SHIFT0, c, h, b * P:(b + 1) * P],
                                             start=True, stop=(c < qb), skip_group_check=True)
                        last = pe.matmul(cols, ident_b[:], causal_qk[:], start=False, stop=True,
                                         skip_group_check=True)
                    last.then_inc(s["max_full"], 1)
                pe.wait_ge(s["max_read"], max_done(qb))
                if qb:
                    pe.wait_ge(s["z_ready"], 2 * EC * qb)
                pe.transpose(pX[:, 0:P], row_max[:], ident[:]).then_inc(s["maxT_full"], 1)

            def image_scores(i):
                qb, b, _ = units[i]
                if b > 0:
                    pe.wait_ge(s["att_step"], 2 * (i // G) - 1)
                for h in range(H):
                    last = pe.matmul(pX[0:H, 0:P], Kdiag[0:ROWS, b, h, :], Qst[0:ROWS, h, b * P:(b + 1) * P],
                                     start=(h == 0), stop=(h == H - 1))
                last.then_inc(s["img_scores"], 1)

            def scores(i):
                qb, b, g = units[i]
                if i >= 2:
                    pe.wait_ge(s["prob_ready"], i - 1)
                ps = pA[i % 2]
                pe.matmul(ps[:, 0, :], ident_b[:], causal_kq[:, None, :].to_broadcast([P, 4, P]),
                          start=True, stop=False, skip_group_check=True)
                for j in range(4):
                    h = 4 * g + j
                    q = Qst[0:ROWS, h, b * P:(b + 1) * P]
                    last = pe.matmul(ps[:, 0, j * P:(j + 1) * P], Kst[0:ROWS, qb, h, b * P:(b + 1) * P], q,
                                     start=False, stop=True, skip_group_check=True)
                    if qb:
                        last = pe.matmul(ps[:, 1, j * P:(j + 1) * P], Kst[0:ROWS, 0, h, b * P:(b + 1) * P], q,
                                         start=True, stop=True, skip_group_check=True)
                last.then_inc(s["score_full"], 1)

            def values(i):
                qb, b, g = units[i]
                if g == 0:
                    pe.wait_ge(s["img_prob"], i // G + 1)
                    if i >= G:
                        pe.wait_ge(s["att_copied"], i // G)
                dst = pV[:, g * P:(g + 1) * P]
                pe.matmul(dst, Vimg[:, b, g, :], prob_img[:], start=True, stop=False, skip_group_check=True)
                pe.wait_ge(s["prob_ready"], i + 1)
                for j in range(4):
                    for c in range(qb + 1):
                        last = pe.matmul(pV[32 * j:32 * j + D + 1, g * P:(g + 1) * P],
                                         V[:, qb if c == 0 else 0, b, 4 * g + j, :],
                                         prob[:, i % 2, c, j * P:(j + 1) * P], start=False, stop=(c == qb),
                                         skip_group_check=True)
                last.then_inc(s["pv_full"], 1)

            def denominators(n):
                pe.wait_ge(s["att_copied"], n + 1)
                pe.wait_ge(s["img_prob"], n + 1)
                pe.matmul(pX[:], sel_den[:], att_raw[:], start=True, stop=True).then_inc(s["den_full"], 1)

            def projection(qb, hf):
                n = 2 * qb + hf
                pe.wait_ge(s["att_step"], 2 * HALF * (n + 1))
                for m in range(EC):
                    if m:
                        pe.wait_ge(s["z_ready"], EC * n + m)
                    for g in range(G):
                        last = pe.matmul(pX[:], w_proj[:, g, m * P:(m + 1) * P],
                                         att[:, g, :, :].rearrange("p b q -> p (b q)"),
                                         start=(g == 0), stop=(g == G - 1))
                    last.then_inc(s["proj_full"], 1)

            wait_tile_empty(pe, len(TILES) - 1)
            wait_tile_empty(pe, len(TILES) - 2)
            pe.wait_ge(s["act_tiles"], tiles_done("act", len(TILES)))
            wait_input("stack_k0", 96)
            wait_input("stack_img", 96)
            wait_input("stack_mask", 16 * TB * H)
            wait_input("in_proj", 64)
            wait_input("ones_k")
            wait_input("ones_q")
            for qb in range(TB):
                wait_input(f"stack_k{qb}", 96)
                wait_input(f"stack_q{qb}", 96)
                maxima(qb)
                pe.wait_ge(s["shift_sent"], 48 * (qb + 1))
                if qb == 0:
                    pe.wait_ge(s["kdiag_ready"], 1)
                    pe.wait_ge(s["vimg_ready"], 2 * B)
                n0 = qb * B * G
                for b in range(B):
                    if b == HALF:
                        pe.wait_ge(s["z_ready"], EC * (2 * qb + 1))
                    image_scores(n0 + b * G)
                    for g in range(G):
                        i = n0 + b * G + g
                        scores(i)
                        if g:
                            values(i - 1)
                    values(n0 + b * G + G - 1)
                    denominators(qb * B + b)
                    if b % HALF == HALF - 1:
                        projection(qb, b // HALF)

            def seed(g, i):
                dst = pG[g % 2][:, 0:GS, :].rearrange("p t (m b) -> p m t b", m=EC)
                if i == 0:
                    pe.wait_ge(s["zq_ready"], EC * (g + 1))
                    pe.wait_ge(s["b_scaled"], 3)
                m = i % 2
                if i < 2:
                    ins = pe.matmul(dst[:, m], b_rec[:, m * P:(m + 1) * P],
                                    ones_row[:].rearrange("p (t b) -> p t b", t=GS), start=(i == 0), stop=False,
                                    skip_group_check=True)
                else:
                    k = i // 2 - 1
                    ins = pe.matmul(dst[:, m], wzT[:, k, m * P:(m + 1) * P], zq[:, g % 2, :, k * B:(k + 1) * B, 0],
                                    start=False, stop=True, skip_group_check=True)
                ins.then_inc(s["seeded"], 1)

            pe.wait_ge(s["h0_ready"], 1)
            pe.wait_ge(s["wh_split"], 6)
            for i in range(6):
                seed(0, i)
            for m in range(EC):
                for k in range(EC):
                    pe.matmul(pG[0][:, 0, m * B:(m + 1) * B], whT[:, k, m * P:(m + 1) * P],
                              Hf[:, 2 * GS - 1, k * B:(k + 1) * B], start=False, stop=True, skip_group_check=True)
            for t in range(S):
                g, st = t // GS, t % GS
                dst = pG[g % 2][:, st, :]
                prev = (t + 1) % 2
                for part, weights in ((H1, (0, 1, 2)), (H2, (0, 1))):
                    if t:
                        pe.wait_ge(s["h_hi" if part is H1 else "h_low"], t)
                    for w in weights:
                        for m in range(EC):
                            for k in range(EC):
                                last = pe.matmul(dst[:, m * B:(m + 1) * B], wh_parts[:, w, k, m * P:(m + 1) * P],
                                                 part[:, prev, k * B:(k + 1) * B], start=False, stop=True,
                                                 skip_group_check=True)
                last.then_inc(s["gate_sum"], 1)
                if g + 1 < NG and 2 <= st < 8:
                    seed(g + 1, st - 2)

            for n in range(TB * B // 2):
                tb, b0 = n // (B // 2), 2 * (n % (B // 2))
                pe.wait_ge(s["y_ready"], EC * (NG // TB) * (tb + 1))
                if n >= 2:
                    pe.wait_ge(s["yt_copied"], n - 1)
                ps = pA[n % 2][:, 0, :]
                for i in range(2):
                    for k in range(EC):
                        last = pe.transpose(ps[:, i * E + k * P:i * E + (k + 1) * P], zT[:, k, tb, b0 + i, :],
                                            ident[:])
                last.then_inc(s["yt_full"], 1)

        @block.scalar
        def _(act):
            nsplit = 0
            for n, (kind, where, who) in enumerate(TILES):
                if who != "act":
                    continue
                act.wait_ge(s["tile_full"], n + 1)
                ps = bank(n)
                if kind == "x":
                    tb, k, hf = where
                    dst = xT[:, k, tb, hf * HALF:(hf + 1) * HALF, :].rearrange("p b q -> p (b q)")
                    act.activation(dst, ps, ACT.Copy).then_inc(s["act_tiles"], 1)
                elif kind == "cond":
                    act.activation(Hf[:, 2 * GS - 1, :], ps[:, 0:STEP], ACT.Copy).then_inc(s["h0_ready"], 1)
                    act.activation(bias_cols[:], ps[:, STEP:STEP + 5 * EC], ACT.Copy).then_inc(s["bias_ready"], 1)
                    act.activation(condT[:].rearrange("p k b -> p (k b)"), ps[:, 0:STEP], ACT.Copy
                                   ).then_inc(s["act_tiles"], 1)
                elif kind in ("uk", "uv", "wz"):
                    dst = {"uk": ukT, "uv": uvT, "wz": wzT}[kind]
                    act.activation(dst[:].rearrange("p k e -> p (k e)"), ps, ACT.Copy).then_inc(s["act_tiles"], 1)
                elif kind == "wh":
                    act.activation(whT[:].rearrange("p k e -> p (k e)"), ps, ACT.Copy, scale=0.5
                                   ).then_inc(s["wh_split"], 1)
                    act.activation(wh_parts[:, 0].rearrange("p k e -> p (k e)"), ps, ACT.Copy, scale=0.5
                                   ).then_inc(s["act_tiles"], 1)
                elif kind in ("k", "q"):
                    tb, m, hf = where
                    c = m if kind == "q" else EC + m
                    scale = 0.25 if kind == "q" else 1.0
                    if nsplit == 0:
                        act.wait_ge(s["b_scaled"], 3)
                    if nsplit >= 2:
                        act.wait_ge(s["kq_mid"], nsplit - 1)
                        act.wait_ge(s["kq_rest"], nsplit - 1)
                        wait_stored(act, nsplit - 2)
                    act.activation(full[:, nsplit % 2], ps, ACT.Identity, bias=b_qk[:, c:c + 1], scale=scale
                                   ).then_inc(s["kq_hi"], 1)
                    ins = act.activation(parts[:, nsplit % 2, 0], ps, ACT.Identity, bias=b_qk[:, c:c + 1], scale=scale)
                    ins.then_inc(s["kq_hi"], 1)
                    act.wait_ge(s["kq_hi"], 2 * (nsplit + 1))
                    act.sem_inc(s["act_tiles"], 1)
                    nsplit += 1
                elif kind == "kimg":
                    for m in range(EC):
                        act.activation(img_full[:, m, :], ps[:, m * B:(m + 1) * B], ACT.Identity, bias=b_uk[:, m:m + 1]
                                       ).then_inc(s["img_hi"], 1)
                    for m in range(EC):
                        ins = act.activation(parts_img[:, 0, m, :], ps[:, m * B:(m + 1) * B], ACT.Identity,
                                             bias=b_uk[:, m:m + 1]).then_inc(s["img_hi"], 1)
                    act.wait_ge(s["img_hi"], 2 * EC)
                    act.sem_inc(s["act_tiles"], 1)

            act.wait_ge(s["kq_mid"], len(SPLITS))
            act.wait_ge(s["kq_rest"], len(SPLITS))
            for i, (qb, b, g) in enumerate(units):
                if g == 0:
                    act.wait_ge(s["img_scores"], i // G + 1)
                    if i:
                        act.wait_ge(s["pv_full"], i)
                    act.activation(prob_img[:], pX[0:H, 0:P], ACT.Exp).then_inc(s["img_prob"], 1)
                act.wait_ge(s["score_full"], i + 1)
                if i >= 2:
                    act.wait_ge(s["pv_full"], i - 1)
                act.activation(prob[:, i % 2, 0:qb + 1, :], pA[i % 2][:, 0:qb + 1, :], ACT.Exp
                               ).then_inc(s["prob_ready"], 1)

            for t in range(S):
                g, st = t // GS, t % GS
                act.wait_ge(s["gate_sum"], t + 1)
                if t >= 2:
                    act.wait_ge(s["arg_ready"], t - 1)
                act.activation(gate[:, t % 2, :, 1], pG[g % 2][:, st, :], ACT.Tanh).then_inc(s["gate_ready"], 1)
                act.wait_ge(s["arg_ready"], t + 1)
                if t >= 2:
                    act.wait_ge(s["h_low"], t - 1)
                act.activation(H1[:, t % 2], arg[:, t % 2, :, 1], ACT.Tanh).then_inc(s["h_hi"], 1)
                if st == 0 and g >= 2:
                    act.wait_ge(s["y_ready"], EC * (g - 1))
                act.activation(Hf[:, t % (2 * GS), :], arg[:, t % 2, :, 1], ACT.Tanh).then_inc(s["h_full"], 1)

        @block.vector
        def _(dve):
            dve.wait_ge(s["in_small"], 16 * 7)
            dve.wait_ge(s["bias_ready"], 1)
            dve.tensor_scalar(b_qk[:, 0:EC], b_qk[:, 0:EC], 0.25, None, ALU.mult).then_inc(s["b_scaled"], 1)
            dve.tensor_scalar(b_rec[:], b_rec[:], 0.5, None, ALU.mult).then_inc(s["b_scaled"], 1)
            dve.tensor_scalar(leak[:], alpha_in[:], -1.0, 1.0, ALU.mult, ALU.add).then_inc(s["b_scaled"], 1)

            dve.wait_ge(s["in_mask"], 16)
            dve.tensor_copy(mask_parts[:, 0, :], mask_in[:]).then_inc(s["mask_p"], 1)
            dve.wait_ge(s["mask_p"], 1)
            dve.tensor_tensor(mask_rest[:], mask_in[:], mask_parts[:, 0, :], ALU.subtract).then_inc(s["mask_p"], 1)
            dve.wait_ge(s["mask_p"], 2)
            dve.tensor_copy(mask_parts[:, 1, :], mask_rest[:]).then_inc(s["mask_p"], 1)
            dve.wait_ge(s["mask_p"], 3)
            dve.tensor_tensor(mask_parts[:, 2, :], mask_rest[:], mask_parts[:, 1, :], ALU.subtract
                              ).then_inc(s["mask_p"], 1)
            dve.wait_ge(s["mask_p"], 4)
            dve.sem_inc(s["mask_p"], 1)

            nsplit = 0
            dve.wait_ge(s["consts"], CONSTS)
            for n, (kind, where, who) in enumerate(TILES):
                ps = bank(n)
                if kind in ("k", "q"):
                    i = nsplit
                    dve.wait_ge(s["kq_hi"], 2 * (i + 1))
                    if i:
                        dve.wait_ge(s["kq_low"], i)
                    dve.tensor_tensor(rest[:], full[:, i % 2], parts[:, i % 2, 0], ALU.subtract
                                      ).then_inc(s["kq_rest"], 1)
                    dve.wait_ge(s["kq_mid"], i + 1)
                    dve.wait_ge(s["kq_rest"], i + 1)
                    dve.tensor_tensor(parts[:, i % 2, 2], rest[:], parts[:, i % 2, 1], ALU.subtract
                                      ).then_inc(s["kq_low"], 1)
                    nsplit += 1
                elif kind == "kimg":
                    dve.wait_ge(s["img_hi"], 2 * EC)
                    dve.tensor_tensor(img_rest[:], img_full[:], parts_img[:, 0], ALU.subtract
                                      ).then_inc(s["img_rest_s"], 1)
                    dve.wait_ge(s["img_rest_s"], 1)
                    dve.tensor_copy(parts_img[:, 1], img_rest[:]).then_inc(s["img_mid"], 1)
                    dve.wait_ge(s["img_mid"], 1)
                    dve.tensor_tensor(parts_img[:, 2], img_rest[:], parts_img[:, 1], ALU.subtract
                                      ).then_inc(s["img_low"], 1)
                elif kind == "v":
                    tb, b0 = where
                    dve.wait_ge(s["tile_full"], n + 1)
                    dve.tensor_tensor(V[:, tb, b0:b0 + 2, :, 0:D],
                                      ps.rearrange("p (b h d) -> p b h d", b=2, h=H),
                                      b_v[:].rearrange("p (h d) -> p h d", h=H)[:, None].to_broadcast([P, 2, H, D]),
                                      ALU.add).then_inc(s["dve_tiles"], 1)
                elif kind == "vimg":
                    dve.wait_ge(s["tile_full"], n + 1)
                    w = wh_rest[0:H, :]
                    if where == 0:
                        dve.wait_ge(s["mask_p"], 5)
                        dve.wait_ge(s["act_tiles"], tiles_done("act", tile_at("x", (1, EC - 1, 1))))
                    if where:
                        dve.wait_ge(s["vimg_ready"], 2 * where)
                    dve.tensor_tensor(w.rearrange("p (b e) -> p b e", b=2), ps[0:H, :].rearrange("p (b e) -> p b e", b=2),
                                      b_uv[:, None, :].to_broadcast([H, 2, E]), ALU.add
                                      ).then_inc(s["dve_tiles"], 1)
                    wait_tile_empty(dve, n)
                    for i in range(2):
                        dst = Vimg[:, where + i].rearrange("p g (j c) -> p (g j) c", j=4)[:, :, 0:D]
                        dve.tensor_tensor(dst, w[:, i * E:(i + 1) * E].rearrange("p (h d) -> p h d", h=H),
                                          own_head[:].rearrange("p (h d) -> p h d", h=H), ALU.mult
                                          ).then_inc(s["vimg_ready"], 1)
                        dst = Vimg[:, where + i].rearrange("p g (j c) -> p (g j) c", j=4)[:, :, D:32]
                        dve.tensor_copy(dst, own_head[:].rearrange("p (h d) -> p h d", h=H)
                                        ).then_inc(s["vimg_ready"], 1)
                elif kind == "wh":
                    dve.wait_ge(s["act_tiles"], tiles_done("act", n))
                    dve.wait_ge(s["wh_split"], 1)
                    dve.wait_ge(s["vimg_ready"], 2 * B)
                    w = [wh_parts[:, i].rearrange("p k e -> p (k e)") for i in range(3)]
                    dve.tensor_tensor(wh_rest[:], whT[:].rearrange("p k e -> p (k e)"), w[0], ALU.subtract
                                      ).then_inc(s["wh_split"], 1)
                    dve.wait_ge(s["wh_split"], 2)
                    dve.tensor_copy(w[1], wh_rest[:]).then_inc(s["wh_split"], 1)
                    dve.wait_ge(s["wh_split"], 3)
                    dve.tensor_tensor(w[2], wh_rest[:], w[1], ALU.subtract).then_inc(s["wh_split"], 3)

            dve.wait_ge(s["stack_img"], 96)
            dve.tensor_copy(Kdiag[0:SLOTS].rearrange("p b h c -> p b (h c)")[:, :, 0:H * H:H + 1],
                            Kimg[:].rearrange("p h b -> p b h")).then_inc(s["kdiag_ready"], 1)

            def maxima(qb):
                for n, (q, b, h0) in enumerate(max_tiles):
                    if q != qb:
                        continue
                    nh = HEADS_OF_TILE[qb]
                    cols = 1 + P * (qb + 1)
                    per = nh // 2
                    src = pA[n % 2][:, :, 0:per * cols].rearrange("p a (h c) -> p a h c", h=per)
                    dve.wait_ge(s["max_full"], n + 1)
                    dve.tensor_reduce(row_max[:].rearrange("p (h b) -> p h b", b=B)[:, h0:h0 + nh, b].rearrange("p (a h) -> p a h", a=2),
                                      src, AX_X, ALU.max).then_inc(s["max_read"], 1)
                dve.wait_ge(s["maxT_full"], qb + 1)
                k = 5 * qb
                if qb:
                    dve.wait_ge(s["shift_sent"], 48)
                dve.tensor_scalar(shift[:], pX[:, 0:P], -1.0, None, ALU.mult).then_inc(s["shift_step"], 1)
                dve.wait_ge(s["shift_step"], k + 1)
                dve.tensor_copy(shift_parts[:, 0], shift[:]).then_inc(s["shift_step"], 1)
                dve.wait_ge(s["shift_step"], k + 2)
                dve.tensor_tensor(shift_rest[:], shift[:], shift_parts[:, 0], ALU.subtract
                                  ).then_inc(s["shift_step"], 1)
                dve.wait_ge(s["shift_step"], k + 3)
                dve.tensor_copy(shift_parts[:, 1], shift_rest[:]).then_inc(s["shift_step"], 1)
                dve.wait_ge(s["shift_step"], k + 4)
                dve.tensor_tensor(shift_parts[:, 2], shift_rest[:], shift_parts[:, 1], ALU.subtract
                                  ).then_inc(s["shift_step"], 1)

            for qb in range(TB):
                maxima(qb)
                for b in range(B):
                    n = qb * B + b
                    dve.wait_ge(s["pv_full"], G * (n + 1))
                    if n:
                        dve.wait_ge(s["den_full"], n)
                        dve.wait_ge(s["att_step"], 2 * n)
                    dve.tensor_copy(att_raw[:], pV[:]).then_inc(s["att_copied"], 1)
                    dve.wait_ge(s["den_full"], n + 1)
                    dve.reciprocal(att_inv[:], pX[:]).then_inc(s["att_step"], 1)
                    dve.wait_ge(s["att_step"], 2 * n + 1)
                    if n >= HALF:
                        dve.wait_ge(s["proj_full"], EC * (n // HALF))
                    dve.tensor_tensor(att[:, :, b % HALF, :], att_raw[:].rearrange("p (g q) -> p g q", g=G),
                                      att_inv[:].rearrange("p (g q) -> p g q", g=G), ALU.mult
                                      ).then_inc(s["att_step"], 1)
                    if b % HALF == HALF - 1:
                        hf = b // HALF
                        for m in range(EC):
                            dve.wait_ge(s["proj_full"], EC * (2 * qb + hf) + m + 1)
                            bs = slice(hf * HALF, (hf + 1) * HALF)
                            dve.scalar_tensor_tensor(zT[:, m, qb, bs, :].rearrange("p b q -> p (b q)"), pX[:],
                                                     b_proj[:, m:m + 1],
                                                     xT[:, m, qb, bs, :].rearrange("p b q -> p (b q)"),
                                                     ALU.add, ALU.add).then_inc(s["z_ready"], 1)

            dve.wait_ge(s["b_scaled"], 3)
            dve.wait_ge(s["h0_ready"], 1)
            for t in range(S):
                g, st = t // GS, t % GS
                prev = (t + 2 * GS - 1) % (2 * GS)
                pair = zq[:, g % 2, st]
                if t:
                    dve.wait_ge(s["h_full"], t)
                    if t >= 2:
                        dve.wait_ge(s["gate_sum"], t)
                    dve.tensor_tensor(H2[:, (t - 1) % 2], Hf[:, prev, :], H1[:, (t - 1) % 2], ALU.subtract
                                      ).then_inc(s["h_low"], 1)
                if st == 0:
                    dve.wait_ge(s["zq_ready"], EC * (g + 1))
                for k in range(EC):
                    c = slice(k * B, (k + 1) * B)
                    dve.scalar_tensor_tensor(pair[:, c, 1], Hf[:, prev, c], leak[:, k:k + 1], pair[:, c, 0],
                                             ALU.mult, ALU.add).then_inc(s["q_ready"], 1)
                dve.wait_ge(s["q_ready"], EC * (t + 1))
                dve.wait_ge(s["gate_ready"], t + 1)
                dve.tensor_tensor_scan(arg[:, t % 2].rearrange("p a b -> p (a b)"),
                                       gate[:, t % 2].rearrange("p a b -> p (a b)"),
                                       pair.rearrange("p a b -> p (a b)"), 0.0, ALU.mult, ALU.add
                                       ).then_inc(s["arg_ready"], 1)

            for n in range(TB * B // 2):
                dve.wait_ge(s["yt_full"], n + 1)
                if n >= 2:
                    dve.wait_ge(s[f"out_sent{n % 2}"], 16 * (n // 2))
                dve.tensor_copy(y_out[:, n % 2].rearrange("p b e -> p (b e)"), pA[n % 2][:, 0, :]
                                ).then_inc(s["yt_copied"], 1)


_INS = ["x", "cond_1024", "mask_Bx1x1xS_ff0", "L0_cond_c_attn_w", "L0_cond_c_attn_b", "L0_cond_c_proj_w",
        "L0_cond_c_proj_b", "L0_cond_uk_w", "L0_cond_uk_b", "L0_cond_uv_w", "L0_cond_uv_b", "L1_cond_W",
        "L1_cond_b", "L1_cond_alpha"]


def kernel(**inputs):
    import numpy as np
    import concourse.bacc as bacc
    from concourse.bass_utils import run_bass_kernel_spmd as run

    nc = bacc.Bacc("TRN2", target_bir_lowering=False, num_devices=1)
    arrays, args = {}, []
    for name in _INS:
        a = np.ascontiguousarray(inputs[name])
        arrays[f"in_{name}"] = a
        args.append(nc.dram_tensor(f"in_{name}", a.shape, mybir.dt.from_np(a.dtype), kind="ExternalInput").ap())
    out = nc.dram_tensor("out_0", (8, 256, 256), F32, kind="ExternalOutput").ap()
    build(nc, *args, out)
    r = run(nc, [arrays], core_ids=[0])
    return r.results[0]["out_0"]
```

```python
import concourse.bass as bass
from concourse import mybir
from contextlib import ExitStack

F32 = mybir.dt.float32
BF16 = mybir.dt.bfloat16
F16 = mybir.dt.float16
ALU = mybir.AluOpType
ACT = mybir.ActivationFunctionType
AX_X = mybir.AxisListType.X

P = 128
HIDDEN_SCORE = -30000.0

PAIRS = [(0, 0), (0, 1), (1, 0), (1, 1), (0, 2), (2, 0)]


def build(nc, x, cond, mask, attn_w, attn_b, proj_w, proj_b, uk_w, uk_b, uv_w, uv_b, rec_w, rec_b, alpha, out):
    B, S, E = x.shape
    H, D = 16, 16
    EC = E // P
    TB = S // P
    G = H // 4
    HALF = B // 2
    NQ = HALF * P
    SLOTS = len(PAIRS) * D
    MASK0, SHIFT0, ROWS = SLOTS, SLOTS + 3, SLOTS + 6
    STEP = EC * B
    GS = 16
    NG = S // GS
    QUARTERS = TB * 2
    BATCHES = TB * B
    UNITS = BATCHES * G
    UNITS_0 = B * G
    EARLY = 2
    FIRST = (B + EARLY) * G
    ATT_STEPS = 4 * (UNITS - FIRST)
    VD = D + 1

    ctx = ExitStack()
    with ctx:
        def sb(name, shape, dt=F32):
            return ctx.enter_context(nc.sbuf_tensor(name, shape, dt))

        def sem(name):
            return ctx.enter_context(nc.semaphore(name))

        def dram(name, shape, dt):
            return nc.dram_tensor(name, shape, dt, kind="Internal").ap()

        xin = sb("xin", [P, TB, B, E])
        region = sb("region", [P, 15 * NQ])

        def view(first, count, pattern=None, **sizes):
            v = region[:, first * NQ:(first + count) * NQ]
            return v.rearrange(pattern, **sizes) if pattern else v

        full = view(0, 2, "p (a n) -> p a n", a=2)
        rest = view(2, 1)
        w_attn = view(3, 3, "p (c e) -> p c e", c=EC)
        w_uk = view(6, 1, "p (c e) -> p c e", c=EC)
        w_uv = view(7, 1, "p (c e) -> p c e", c=EC)
        ukT = view(8, 1, "p (c e) -> p c e", c=EC)
        uvT = view(9, 2, "p (c n) -> p c n", c=EC)
        parts = view(11, 3).bitcast(BF16).rearrange("p (a i n) -> p a i n", a=2, i=3)
        prob = view(0, 4, "p (a c n) -> p a c n", a=2, c=2)
        att = view(4, 8, "p (a g b q) -> p a g b q", a=2, g=G, b=HALF)
        att_raw = view(12, 1)
        prob_img = view(13, 1)
        att_inv = view(14, 1)
        y_out = view(0, 2, "p (a b e) -> p a b e", a=2, b=2)
        w_proj = sb("w_proj", [P, G, E])
        w_rec = sb("w_rec", [P, EC, 2 * E])
        cond_in = sb("cond_in", [B, E])
        bias_rows = sb("bias_rows", [5 * EC, P])
        bias_cols = sb("bias_cols", [P, 5 * EC])
        b_qk, b_uk = bias_cols[:, 0:2 * EC], bias_cols[:, 2 * EC:3 * EC]
        b_proj, alpha_in = bias_cols[:, 3 * EC:4 * EC], bias_cols[:, 4 * EC:5 * EC]
        b_v = sb("b_v", [P, E])
        b_uv = sb("b_uv", [1, G * P])
        b_rec = sb("b_rec", [1, E])
        ident = sb("ident", [P, P])
        ident_b = sb("ident_b", [P, P], BF16)
        causal_qk = sb("causal_qk", [P, P], BF16)
        causal_kq = sb("causal_kq", [P, P], BF16)
        ones_row = sb("ones_row", [1, P])
        sel_den = sb("sel_den", [P, P])

        xT = sb("xT", [P, EC, TB, B, P])
        zT = xT
        condT = sb("condT", [P, EC, B])
        parts_img = sb("parts_img", [P, 3, EC, B], BF16)
        img_full = sb("img_full", [P, EC, B])
        img_rest = sb("img_rest", [P, EC, B])
        mask_parts = sb("mask_parts", [B, 3, S], BF16)
        Kst = sb("Kst", [P, TB, H, B * P], BF16)
        Qst = sb("Qst", [P, 2, H, NQ], BF16)
        Qbuf = [Qst[:, 0], Qst[:, 1], xin[:].rearrange("p t b e -> p (t b e)").bitcast(BF16).rearrange(
            "p (h n) -> p h n", h=H)]
        Kimg = sb("Kimg", [P, H, B], BF16)
        Vimg = sb("Vimg", [P, G, B])
        Vflat = sb("V", [P, TB * B * H * VD + 32 - VD])
        V = Vflat[:, 0:TB * B * H * VD].rearrange("p (t b h d) -> p t b h d", t=TB, b=B, h=H)
        row_max = sb("row_max", [P, 2, H * HALF])
        shift = sb("shift", [H * HALF, P])
        shift_rest = sb("shift_rest", [H * HALF, P])
        shift_parts = sb("shift_parts", [H * HALF, 3, P], BF16)

        whT = sb("whT", [P, EC, E])
        wzT = sb("wzT", [P, EC, E])
        wh_rest = sb("wh_rest", [P, EC * E])
        mask_in, mask_rest = wh_rest[0:B, 0:S], wh_rest[0:B, S:2 * S]
        wh_parts = sb("wh_parts", [P, 3, EC, E], BF16)
        leak = sb("leak", [P, EC])
        zq = w_rec[:].rearrange("p c e -> p (c e)").rearrange("p (a t c i) -> p a t c i", a=2, t=GS, i=2)
        Hf = sb("Hf", [P, 2 * GS, STEP])
        ones_rows = Hf[0:3, 0:GS].rearrange("p t c -> p (t c)").bitcast(BF16)
        H1 = sb("H1", [P, 2, STEP], F16)
        H2 = sb("H2", [P, 2, STEP], F16)
        gate = sb("gate", [P, 2, STEP, 2])
        arg = sb("arg", [P, 2, STEP, 2])

        def psum(name, shape):
            return ctx.enter_context(nc.psum_tensor(name, shape, F32))

        pG = psum("pG", [P, 2, 512])
        pS = psum("pS", [P, 2, 512])
        pP = psum("pP", [P, 512])
        pI = psum("pI", [P, 512])
        pV = psum("pV", [P, 512])
        pX = psum("pX", [P, 512])

        scr = {"k": dram("scr_k", [3, E, TB, B * P], BF16), "q": dram("scr_q", [3, E, TB, B * P], BF16)}
        scr_img = dram("scr_img", [3, E, B], BF16)
        scr_mask = dram("scr_mask", [3, TB, B * P], BF16)

        names = """in_x0a in_x0b in_x1 in_cond in_uk in_attn in_small in_uv in_rec in_mask in_proj consts
            tile_full act_tiles dve_tiles kq_hi kq_mid kq_rest kq_low kq_stored0 kq_stored1
            img_hi img_rest_s img_mid img_low img_stored img_stacked vimg_ready
            mask_p mask_stored mask_stacked ones_k ones_q ones_q2
            stack_k0 stack_k1 stack_k2 stack_k3 stack_q0 stack_q1 stack_q2 stack_q3
            ring_full ring_read shift_step shift_sent
            score_full prob_ready pv_full img_full_s img_prob raw_ready den_full inv_ready att_ready proj_full z_ready
            wh_split bias_ready b_scaled h0_ready zq_ready y_ready seeded gate_sum gate_ready h_hi h_full h_low
            q_ready arg_ready yt_full yt_copied out_sent0 out_sent1""".split()
        s = {n: sem(n) for n in names}
        CONSTS = 19

        block = ctx.enter_context(nc.Block())

        def x_tiles(tb):
            return [("x", (tb, k, hf), "act") for hf in range(2) for k in range(EC)]

        def kq_tiles(kind, tb):
            return [(kind, (tb, m, hf), "act") for hf in range(2) for m in range(EC)]

        def v_tiles(tb):
            return [("v", (tb, b), "dve") for b in range(0, B, 2)]

        TILES_A = (x_tiles(0) + [("cond", (), "act")] + kq_tiles("k", 0) + kq_tiles("q", 0)
                   + [("uk", (), "act"), ("kimg", (), "act"), ("uv", (), "act"), ("vimg", (), "dve")]
                   + v_tiles(0) + x_tiles(1) + kq_tiles("k", 1))
        TILES_B = kq_tiles("q", 1) + v_tiles(1) + [("wh", (), "act"), ("wz", (), "act")]
        TILES = TILES_A + TILES_B
        BANKS = 4

        def bank(n):
            return [pS[:, 0, :], pS[:, 1, :], pP[:], pI[:]][n % BANKS]

        def tiles_done(engine, n):
            return sum(t[2] == engine for t in TILES[:n + 1])

        def wait_tile_empty(eng, n):
            who = TILES[n][2]
            eng.wait_ge(s[f"{who}_tiles"], tiles_done(who, n))

        def tile_at(kind, where=None):
            return next(n for n, t in enumerate(TILES) if t[0] == kind and (where is None or t[1] == where))

        SPLITS = [t for t in TILES if t[0] in "kq"]
        SPLIT_OF = {n: i for i, n in enumerate(n for n, t in enumerate(TILES) if t[0] in "kq")}

        def wait_stored(eng, n):
            eng.wait_ge(s[f"kq_stored{n % 2}"], 16 * (n // 2 + 1))

        RING = []
        for w in range(QUARTERS):
            nh = 2 - w // 2
            RING += [("max", w, (w % 2) * HALF + b, h, nh) for b in range(HALF) for h in range(0, H, nh)]
            RING.append(("turn", w))

        def ring_at(w):
            return RING.index(("turn", w))

        def ring_beside_tile(n):
            share = -(-(ring_at(1) + 1) // len(TILES_B))
            return range(min(n * share, ring_at(1) + 1), min((n + 1) * share, ring_at(1) + 1))

        def ring_beside_unit(i):
            for w, first in ((2, 2), (3, 20)):
                lo, hi = ring_at(w - 1) + 1, ring_at(w) + 1
                share = 5
                if first <= i < first + 14:
                    return range(min(lo + (i - first) * share, hi), min(lo + (i - first + 1) * share, hi))
            return range(0)

        def probs_done(i):
            return i + 1 + max(0, i + 1 - UNITS_0)

        def batch_of(n):
            return n // B, n % B

        def steps_of(t):
            i = FIRST + t // 4
            return i, t % 4, i // G, i % G

        PROJ_AT = {(3 * HALF + 1) * 4 * G - 4 * FIRST + 3 * p: (2, p) for p in range(8)}
        PROJ_AT |= {ATT_STEPS + 9 + p: (3, p) for p in range(8)}
        Z_AT = {}
        for t_, (w_, p_) in PROJ_AT.items():
            if p_ % G == G - 1:
                Z_AT |= {t_ + 1: (w_, p_ // G, 0), t_ + (3 if w_ == 2 else 2): (w_, p_ // G, 1)}
        SEED_FROM = 8
        YT_FIRST = S // 2 + 24

        @block.sync
        def _(sp):
            def rows_of(b0, b1, tb):
                return x[b0:b1, tb * P:(tb + 1) * P, :].rearrange("b p e -> p b e")
            sp.dma_start(xin[:, 0, 0:HALF], rows_of(0, HALF, 0)).then_inc(s["in_x0a"], 16)
            sp.dma_start(xin[:, 0, HALF:B], rows_of(HALF, B, 0)).then_inc(s["in_x0b"], 16)
            sp.dma_start(w_attn, attn_w.rearrange("(c p) e -> p c e", p=P)).then_inc(s["in_attn"], 16)
            sp.dma_start(cond_in[:], cond).then_inc(s["in_cond"], 16)
            for row, vec in ((0, attn_b[0:2 * E]), (2 * EC, uk_b), (3 * EC, proj_b), (4 * EC, alpha)):
                rows = vec.rearrange("(m p) -> m p", p=P)
                sp.dma_start(bias_rows[row:row + rows.shape[0]], rows).then_inc(s["in_small"], 16)
            sp.dma_start(b_v[:], attn_b[2 * E:3 * E].rearrange("(a e) -> a e", a=1).to_broadcast([P, E])
                         ).then_inc(s["in_small"], 16)
            sp.dma_start(b_rec[:], rec_b.rearrange("(a e) -> a e", a=1)).then_inc(s["in_small"], 16)
            sp.dma_start(mask_in, mask.rearrange("b i j k -> (b i j) k")).then_inc(s["in_mask"], 16)
            sp.dma_start(w_uk, uk_w.rearrange("(c p) e -> p c e", p=P)).then_inc(s["in_uk"], 16)
            sp.wait_ge(s["consts"], CONSTS)
            sp.dma_start(b_uv[:].rearrange("a (h c) -> a h c", c=32)[:, :, 0:D],
                         uv_b.rearrange("(a h d) -> a h d", a=1, d=D)).then_inc(s["in_small"], 16)
            sp.dma_start(w_uv, uv_w.rearrange("(c p) e -> p c e", p=P)).then_inc(s["in_uv"], 16)
            sp.dma_start(xin[:, 1], rows_of(0, B, 1)).then_inc(s["in_x1"], 16)

            ones_n = 2 * GS * STEP

            def ones(dst, name):
                n = dst.free_size() // ones_n if hasattr(dst, "free_size") else None
                sp.dma_start(dst, ones_rows[:, None, :].to_broadcast([3, dst.shape[1], ones_n])).then_inc(s[name], 16)

            ones(Kst[SHIFT0:SHIFT0 + 3].rearrange("i t h (c n) -> i (t h c) n", n=ones_n), "ones_k")
            ones(Qst[MASK0:MASK0 + 3].rearrange("i a h (c n) -> i (a h c) n", n=ones_n), "ones_q")

            def store_split(n):
                kind, (tb, m, hf), _ = SPLITS[n]
                sp.wait_ge(s["kq_hi"], 2 * (n + 1))
                sp.wait_ge(s["kq_mid"], n + 1)
                sp.wait_ge(s["kq_low"], n + 1)
                sp.dma_start(scr[kind][:, m * P:(m + 1) * P, tb, hf * NQ:(hf + 1) * NQ].rearrange("i p n -> p i n"),
                             parts[:, n % 2]).then_inc(s[f"kq_stored{n % 2}"], 16)

            def stack(kind, tb, hf):
                w = 2 * tb + hf
                last = max(n for n, t in enumerate(SPLITS) if t[0] == kind and t[1][0] == tb and t[1][2] == hf)
                wait_stored(sp, last)
                wait_stored(sp, last - 1)
                cols = slice(hf * NQ, (hf + 1) * NQ)
                for i, (pq, pk) in enumerate(PAIRS):
                    src = scr[kind][pk if kind == "k" else pq, :, tb, cols].rearrange("(h d) n -> d h n", d=D)
                    to = slice(i * D, (i + 1) * D)
                    dst = Kst[to, tb, :, cols] if kind == "k" else Qbuf[w % 3][to]
                    sp.dma_start(dst, src).then_inc(s[f"stack_{kind}{w}"], 16)

            for n in range(4):
                store_split(n)
            stack("k", 0, 0)
            store_split(4)
            store_split(5)
            stack("k", 0, 1)
            store_split(6)
            store_split(7)
            stack("q", 0, 0)
            sp.wait_ge(s["mask_p"], 4)
            for i in range(3):
                sp.dma_start(scr_mask[i].rearrange("t (b q) -> b t q", b=B),
                             mask_parts[:, i, :].rearrange("b (t q) -> b t q", t=TB)).then_inc(s["mask_stored"], 16)
            sp.wait_ge(s["img_low"], 1)
            for m in range(EC):
                sp.dma_start(scr_img[:, m * P:(m + 1) * P, :].rearrange("i p b -> p i b"), parts_img[:, :, m, :]
                             ).then_inc(s["img_stored"], 16)
            stack("q", 0, 1)
            sp.wait_ge(s["mask_stored"], 48)
            for tb in range(TB):
                sp.dma_start(Kst[MASK0:MASK0 + 3, tb], scr_mask[:, tb][:, None, :].to_broadcast([3, H, B * P])
                             ).then_inc(s["mask_stacked"], 16)
            sp.wait_ge(s["img_stored"], 16 * EC)
            for i, (pq, pk) in enumerate(PAIRS):
                sp.dma_start(Kimg[i * D:(i + 1) * D], scr_img[pk].rearrange("(h d) b -> d h b", d=D)
                             ).then_inc(s["img_stacked"], 16)
            for j in range(4):
                sp.dma_start(w_proj[32 * j:32 * j + D], proj_w.rearrange("(g j d) n -> j d g n", g=G, j=4)[j]
                             ).then_inc(s["in_proj"], 16)
            sp.dma_start(w_rec[:], rec_w.rearrange("(c p) e -> p c e", p=P)).then_inc(s["in_rec"], 16)
            for n in range(8, 11):
                store_split(n)
            wait_tile_empty(sp, tile_at("x", (1, EC - 1, 1)))
            ones(Qbuf[2][MASK0:MASK0 + 3].rearrange("i h (c n) -> i (h c) n", n=ones_n), "ones_q2")
            store_split(11)
            stack("k", 1, 0)
            store_split(12)
            store_split(13)
            stack("k", 1, 1)
            store_split(14)
            store_split(15)
            stack("q", 1, 0)
            sp.wait_ge(s["score_full"], UNITS_0 // 2)
            sp.wait_ge(s["img_full_s"], HALF)
            stack("q", 1, 1)

            for n in range(BATCHES // 2):
                tb, b = n // (B // 2), 2 * (n % (B // 2))
                sp.wait_ge(s["yt_copied"], n + 1)
                sp.dma_start(out[b:b + 2, tb * P:(tb + 1) * P, :].rearrange("b p e -> p b e"),
                             y_out[:, n % 2]).then_inc(s[f"out_sent{n % 2}"], 16)
            for half in range(2):
                sp.wait_ge(s[f"out_sent{half}"], 16 * (BATCHES // 4))

        @block.gpsimd
        def _(pool):
            n = 0

            def step(ins):
                ins.then_inc(s["consts"], 1)
                pool.wait_ge(s["consts"], n + 1)
                return 1
            n += step(pool.memset(ident[:], 0.0))
            n += step(pool.affine_select(out=ident[:], in_=ident[:], compare_op=ALU.not_equal, fill=1.0, base=0,
                                         pattern=[[-1, P]], channel_multiplier=1))
            n += step(pool.memset(b_uv[:], 1.0))
            n += step(pool.memset(uvT, 0.0))
            n += step(pool.memset(ones_rows, 1.0))
            n += step(pool.memset(w_proj[:], 0.0))
            n += step(pool.memset(Vflat[:], 1.0))
            n += step(pool.memset(ones_row[:], 1.0))
            n += step(pool.memset(sel_den[:], 0.0))
            sel = sel_den[:].rearrange("p (j c) -> p j c", j=4)
            n += step(pool.affine_select(out=sel, in_=sel, compare_op=ALU.not_equal, fill=1.0, base=-D,
                                         pattern=[[-32, 4], [0, 32]], channel_multiplier=1))
            n += step(pool.tensor_copy(ident_b[:], ident[:]))
            n += step(pool.memset(causal_qk[:], 0.0))
            n += step(pool.affine_select(out=causal_qk[:], in_=causal_qk[:], compare_op=ALU.is_ge,
                                         fill=HIDDEN_SCORE, base=0, pattern=[[-1, P]], channel_multiplier=1))
            n += step(pool.memset(causal_kq[:], 0.0))
            n += step(pool.affine_select(out=causal_kq[:], in_=causal_kq[:], compare_op=ALU.is_ge,
                                         fill=HIDDEN_SCORE, base=0, pattern=[[1, P]], channel_multiplier=-1))
            n += step(pool.memset(Kimg[SLOTS:P], 1.0))
            n += step(pool.affine_select(out=Kimg[SLOTS:P], in_=Kimg[SLOTS:P], compare_op=ALU.is_ge, fill=0.0,
                                         base=-(SHIFT0 - SLOTS), pattern=[[0, H], [0, B]], channel_multiplier=1))
            n += step(pool.memset(gate[:], 0.0))
            n += step(pool.memset(H1[:, 1], 0.0))
            assert n == CONSTS

            for i in range(len(SPLITS)):
                pool.wait_ge(s["kq_hi"], 2 * (i + 1))
                if i >= 2:
                    wait_stored(pool, i - 2)
                pool.tensor_tensor(parts[:, i % 2, 1], full[:, i % 2], parts[:, i % 2, 0], ALU.subtract
                                   ).then_inc(s["kq_mid"], 1)

            for w in range(QUARTERS):
                pool.wait_ge(s["shift_step"], 5 * (w + 1))
                for i in range(3):
                    pool.dma_start(Qbuf[w % 3][SHIFT0 + i:SHIFT0 + i + 1].rearrange("o h (b q) -> o (h b) q", b=HALF),
                                   shift_parts[:, i, :]).then_inc(s["shift_sent"], 16)
                if w == QUARTERS - 1:
                    continue

            def halve(g):
                tb, q0 = (g * GS) // P, (g * GS) % P
                if g >= 2:
                    pool.wait_ge(s["arg_ready"], GS * (g - 1))
                    pool.wait_ge(s["seeded"], 6 * (g - 1))
                pool.wait_ge(s["z_ready"], 4 * EC * (tb + 1))
                for k in range(EC):
                    src = zT[:, k, tb, :, q0:q0 + GS].rearrange("p b q -> p q b")
                    pool.tensor_scalar(zq[:, g % 2, :, k * B:(k + 1) * B, 0], src, 0.5, None, ALU.mult
                                       ).then_inc(s["zq_ready"], 1)

            def add_z(g):
                tb, q0 = (g * GS) // P, (g * GS) % P
                pool.wait_ge(s["h_full"], GS * (g + 1))
                pool.wait_ge(s["zq_ready"], EC * (g + 1))
                for k in range(EC):
                    z = zT[:, k, tb, :, q0:q0 + GS].rearrange("p b q -> p q b")
                    h = Hf[:, (g % 2) * GS:(g % 2 + 1) * GS, k * B:(k + 1) * B]
                    pool.tensor_tensor(z, z, h, ALU.add).then_inc(s["y_ready"], 1)

            halve(0)
            halve(1)
            for g in range(NG):
                if g + 2 < NG:
                    pool.wait_ge(s["h_full"], GS * (g + 1))
                    halve(g + 2)
                add_z(g)

        @block.tensor
        def _(pe):
            pe.wait_ge(s["consts"], 2)
            seen = set()

            def wait_once(name, value=16):
                if (name, value) not in seen:
                    seen.add((name, value))
                    pe.wait_ge(s[name], value)

            def first_stage(n):
                kind, where, who = TILES[n]
                if n >= BANKS:
                    wait_tile_empty(pe, n - BANKS)
                ps = bank(n)
                if kind == "x":
                    tb, k, hf = where
                    wait_once("in_x1" if tb else "in_x0" + "ab"[hf])
                    for i in range(HALF):
                        last = pe.transpose(ps[:, i * P:(i + 1) * P], xin[:, tb, hf * HALF + i, k * P:(k + 1) * P],
                                            ident[:])
                elif kind == "cond":
                    wait_once("in_cond")
                    wait_once("consts", CONSTS)
                    wait_once("in_small", 16 * 7)
                    pe.transpose(ps[:, STEP:STEP + 5 * EC], bias_rows[:], ident[0:5 * EC, 0:5 * EC])
                    for k in range(EC):
                        last = pe.transpose(ps[:, k * B:(k + 1) * B], cond_in[:, k * P:(k + 1) * P], ident[0:B, 0:B])
                elif kind in ("uk", "uv", "wh", "wz"):
                    wait_once("in_rec" if kind[0] == "w" else "in_" + kind)
                    w, o = {"uk": (w_uk, 0), "uv": (w_uv, 0), "wh": (w_rec, 0), "wz": (w_rec, E)}[kind]
                    for k in range(EC):
                        for m in range(EC):
                            last = pe.transpose(ps[:, k * E + m * P:k * E + (m + 1) * P],
                                                w[:, m, o + k * P:o + (k + 1) * P], ident[:])
                elif kind in ("k", "q"):
                    tb, m, hf = where
                    wait_once("in_attn")
                    wait_tile_empty(pe, tile_at("x", (tb, EC - 1, hf)))
                    o = (0 if kind == "q" else E) + m * P
                    for k in range(EC):
                        last = pe.matmul(ps, w_attn[:, k, o:o + P],
                                         xT[:, k, tb, hf * HALF:(hf + 1) * HALF, :].rearrange("p b q -> p (b q)"),
                                         start=(k == 0), stop=(k == EC - 1))
                elif kind == "kimg":
                    wait_tile_empty(pe, tile_at("uk"))
                    for m in range(EC):
                        for k in range(EC):
                            last = pe.matmul(ps[:, m * B:(m + 1) * B], ukT[:, k, m * P:(m + 1) * P], condT[:, k, :],
                                             start=(k == 0), stop=(k == EC - 1), skip_group_check=True)
                elif kind == "v":
                    tb, b0 = where
                    for i in range(2):
                        for k in range(EC):
                            last = pe.matmul(ps[:, i * E:(i + 1) * E], xT[:, k, tb, b0 + i, :],
                                             w_attn[:, k, 2 * E:3 * E], start=(k == 0), stop=(k == EC - 1),
                                             skip_group_check=True)
                elif kind == "vimg":
                    wait_tile_empty(pe, tile_at("uv"))
                    for g in range(G):
                        dst = ps[:, g * B:(g + 1) * B]
                        pe.matmul(dst, b_uv[:, g * P:(g + 1) * P], ones_row[:, 0:B], start=True, stop=False,
                                  skip_group_check=True)
                        for k in range(EC):
                            last = pe.matmul(dst, uvT[:, k, g * P:(g + 1) * P], condT[:, k, :],
                                             start=False, stop=(k == EC - 1), skip_group_check=True)
                last.then_inc(s["tile_full"], 1)

            def ring(n):
                kind, w = RING[n][:2]
                qb = w // 2
                ps = pG[:, n % 2, :]
                if kind == "turn":
                    pe.wait_ge(s["ring_read"], n)
                    pe.transpose(ps[0:H * HALF, 0:P], row_max[:, w % 2, :], ident[:]).then_inc(s["ring_full"], 1)
                    return
                _, _, b, h0, nh = RING[n]
                wait_once(f"stack_k{w}", 96)
                if w == 3:
                    wait_once("stack_k2", 96)
                wait_once(f"stack_q{w}", 96)
                if n >= 2:
                    pe.wait_ge(s["ring_read"], n - 1)
                cols = 1 + P * (qb + 1)
                for j in range(nh):
                    h = h0 + j
                    lhs = Qbuf[w % 3][:, h, (b % HALF) * P:(b % HALF + 1) * P]
                    pe.matmul(ps[:, j * cols:j * cols + 1], lhs[0:SLOTS], Kimg[0:SLOTS, h, b:b + 1],
                              start=True, stop=True, skip_group_check=True)
                    for c in range(qb + 1):
                        dst = ps[:, j * cols + 1 + c * P:j * cols + 1 + (c + 1) * P]
                        pe.matmul(dst, lhs[0:SHIFT0], Kst[0:SHIFT0, c, h, b * P:(b + 1) * P],
                                  start=True, stop=(c < qb), skip_group_check=True)
                    last = pe.matmul(dst, ident_b[:], causal_qk[:], start=False, stop=True, skip_group_check=True)
                last.then_inc(s["ring_full"], 1)

            def queries(n, h):
                w = n // HALF
                return Qbuf[w % 3][0:ROWS, h, (n % HALF) * P:(n % HALF + 1) * P]

            def image_scores(n):
                qb, b = batch_of(n)
                if n:
                    pe.wait_ge(s["img_prob"], n)
                wait_once("shift_sent", 48 * (n // HALF + 1))
                for h in range(H):
                    j, g = h % 4, h // 4
                    last = pe.matmul(pI[32 * j:32 * j + 32, g * P:(g + 1) * P],
                                     Kimg[0:ROWS, h, b:b + 1].to_broadcast([ROWS, 32]), queries(n, h),
                                     start=True, stop=True, skip_group_check=True)
                last.then_inc(s["img_full_s"], 1)

            def scores(i):
                n, g = i // G, i % G
                qb, b = batch_of(n)
                if i >= 2:
                    pe.wait_ge(s["prob_ready"], probs_done(i - 1 if qb else i - 2))
                wait_once("shift_sent", 48 * (n // HALF + 1))
                own = 0 if qb else i % 2
                pe.matmul(pS[:, own, :], ident_b[:], causal_kq[:, None, :].to_broadcast([P, 4, P]),
                          start=True, stop=False, skip_group_check=True)
                for j in range(4):
                    h = 4 * g + j
                    last = pe.matmul(pS[:, own, j * P:(j + 1) * P], Kst[0:ROWS, qb, h, b * P:(b + 1) * P],
                                     queries(n, h), start=False, stop=True, skip_group_check=True)
                    if qb:
                        last = pe.matmul(pS[:, 1, j * P:(j + 1) * P], Kst[0:ROWS, 0, h, b * P:(b + 1) * P],
                                         queries(n, h), start=True, stop=True, skip_group_check=True)
                last.then_inc(s["score_full"], 1)

            def values(i, heads=range(4)):
                n, g = i // G, i % G
                qb, b = batch_of(n)
                if heads[0] == 0:
                    if g == 0 and n:
                        pe.wait_ge(s["raw_ready"], G * n)
                    pe.wait_ge(s["prob_ready"], probs_done(i))
                for j in heads:
                    for c in range(qb + 1):
                        first = (((qb if c == 0 else 0) * B + b) * H + 4 * g + j) * VD
                        last = pe.matmul(pV[32 * j:32 * j + 32, g * P:(g + 1) * P], Vflat[:, first:first + 32],
                                         prob[:, i % 2, c, j * P:(j + 1) * P], start=(c == 0), stop=(c == qb),
                                         skip_group_check=True)
                if heads[-1] == 3:
                    last.then_inc(s["pv_full"], 1)

            def denominators(n):
                pe.wait_ge(s["raw_ready"], G * (n + 1))
                if n:
                    pe.wait_ge(s["inv_ready"], 8 * n)
                pe.matmul(pX[:], sel_den[:], att_raw, start=True, stop=True).then_inc(s["den_full"], 1)

            def projection(w, p):
                m, g = p // G, p % G
                ps = pI if (w, m) == (QUARTERS - 1, 1) else pP
                if p == 0:
                    pe.wait_ge(s["att_ready"], G * HALF * (w + 1))
                if g == 0:
                    if (w, m) == (QUARTERS - 1, 1):
                        pe.wait_ge(s["img_prob"], BATCHES)
                    elif w or m:
                        pe.wait_ge(s["z_ready"], 2 * (EC * w + m))
                ins = pe.matmul(ps[:], w_proj[:, g, m * P:(m + 1) * P],
                                att[:, w % 2, g, :, :].rearrange("p b q -> p (b q)"),
                                start=(g == 0), stop=(g == G - 1))
                if g == G - 1:
                    ins.then_inc(s["proj_full"], 1)

            for n in range(len(TILES_A)):
                first_stage(n)
            wait_once("ones_k")
            wait_once("ones_q")
            wait_once("mask_stacked", 16 * TB)
            wait_once("img_stacked", 96)
            for n in range(len(TILES_B)):
                first_stage(len(TILES_A) + n)
                for r in ring_beside_tile(n):
                    ring(r)
            pe.wait_ge(s["act_tiles"], tiles_done("act", len(TILES)))
            pe.wait_ge(s["dve_tiles"], tiles_done("dve", len(TILES)))
            wait_once("in_proj", 64)
            wait_once("ones_q2")

            for i in range(FIRST):
                n, g = i // G, i % G
                scores(i)
                for r in ring_beside_unit(i):
                    ring(r)
                if i:
                    values(i - 1)
                if g == 1 and n:
                    denominators(n - 1)
                if g == 2:
                    image_scores(n)
                if g == 3 and n % HALF == 0 and n:
                    for p in range(EC * G):
                        projection(n // HALF - 1, p)

            def seed(g, i):
                dst = pG[:, g % 2, 0:GS * STEP].rearrange("p (t m b) -> p m t b", t=GS, m=EC)
                if i == 0:
                    pe.wait_ge(s["zq_ready"], EC * (g + 1))
                    pe.wait_ge(s["b_scaled"], 3)
                m = i % 2
                if i < 2:
                    ins = pe.matmul(dst[:, m], b_rec[:, m * P:(m + 1) * P],
                                    ones_row[:].rearrange("p (t b) -> p t b", t=GS), start=(i == 0), stop=False,
                                    skip_group_check=True)
                else:
                    k = i // 2 - 1
                    ins = pe.matmul(dst[:, m], wzT[:, k, m * P:(m + 1) * P], zq[:, g % 2, :, k * B:(k + 1) * B, 0],
                                    start=False, stop=True, skip_group_check=True)
                ins.then_inc(s["seeded"], 1)

            pe.wait_ge(s["h0_ready"], 1)
            pe.wait_ge(s["wh_split"], 6)
            pe.wait_ge(s["ring_read"], len(RING))
            for i in range(6):
                seed(0, i)
            for m in range(EC):
                for k in range(EC):
                    last = pe.matmul(pG[:, 0, m * B:(m + 1) * B], whT[:, k, m * P:(m + 1) * P],
                                     Hf[:, 2 * GS - 1, k * B:(k + 1) * B], start=False, stop=True,
                                     skip_group_check=True)
            last.then_inc(s["gate_sum"], 1)

            def step_gates(t):
                g, st = t // GS, t % GS
                prev = (t + 1) % 2
                for part, ready, weights in ((H1, "h_hi", (0, 1, 2)), (H2, "h_low", (0, 1))):
                    pe.wait_ge(s[ready], t)
                    for w in weights:
                        for m in range(EC):
                            dst = pG[:, g % 2, st * STEP + m * B:st * STEP + (m + 1) * B]
                            for k in range(EC):
                                last = pe.matmul(dst, wh_parts[:, w, k, m * P:(m + 1) * P],
                                                 part[:, prev, k * B:(k + 1) * B], start=False, stop=True,
                                                 skip_group_check=True)
                last.then_inc(s["gate_sum"], 1)

            def rows_back(n, i):
                tb, b0 = n // (B // 2), 2 * (n % (B // 2))
                if i == 0:
                    pe.wait_ge(s["y_ready"], EC * (NG // TB) * (tb + 1))
                    if n >= 2:
                        pe.wait_ge(s["yt_copied"], n - 1)
                    else:
                        pe.wait_ge(s["prob_ready"], probs_done(UNITS - 1))
                ps = pS[:, n % 2, :]
                for k in range(EC):
                    last = pe.transpose(ps[:, i * E + k * P:i * E + (k + 1) * P], zT[:, k, tb, b0 + i, :], ident[:])
                if i:
                    last.then_inc(s["yt_full"], 1)

            for t in range(S):
                g, st = t // GS, t % GS
                if t:
                    step_gates(t)
                if t < ATT_STEPS + 2:
                    i, phase, n, ug = steps_of(t)
                    if phase == 0 and i < UNITS:
                        scores(i)
                    if phase == (1 if i < UNITS else 0):
                        values(i - 1, range(0, 2))
                    if phase == (2 if i < UNITS else 1):
                        values(i - 1, range(2, 4))
                    if phase == 3 and ug == 0:
                        image_scores(n)
                    if phase == 3 and ug == 1:
                        denominators(n - 1)
                if t == ATT_STEPS + 4:
                    denominators(BATCHES - 1)
                if t in PROJ_AT:
                    projection(*PROJ_AT[t])
                if g + 1 < NG and SEED_FROM <= st < SEED_FROM + 6:
                    seed(g + 1, st - SEED_FROM)
                if 0 <= t - YT_FIRST < 4 * (B // 2) and (t - YT_FIRST) % 4 < 2:
                    rows_back((t - YT_FIRST) // 4, (t - YT_FIRST) % 4)
            for n in range(B // 2, BATCHES // 2):
                for i in range(2):
                    rows_back(n, i)

        @block.scalar
        def _(act):
            for n, (kind, where, who) in enumerate(TILES):
                if who != "act":
                    continue
                act.wait_ge(s["tile_full"], n + 1)
                ps = bank(n)
                if kind == "x":
                    tb, k, hf = where
                    dst = xT[:, k, tb, hf * HALF:(hf + 1) * HALF, :].rearrange("p b q -> p (b q)")
                    act.activation(dst, ps, ACT.Copy).then_inc(s["act_tiles"], 1)
                elif kind == "cond":
                    act.activation(bias_cols[:], ps[:, STEP:STEP + 5 * EC], ACT.Copy).then_inc(s["bias_ready"], 1)
                    act.activation(Hf[:, 2 * GS - 1, :], ps[:, 0:STEP], ACT.Copy).then_inc(s["h0_ready"], 1)
                    act.activation(condT[:].rearrange("p k b -> p (k b)"), ps[:, 0:STEP], ACT.Copy
                                   ).then_inc(s["act_tiles"], 1)
                elif kind in ("uk", "wz"):
                    dst = {"uk": ukT, "wz": wzT}[kind]
                    act.activation(dst[:].rearrange("p k e -> p (k e)") if kind == "wz"
                                   else dst.rearrange("p k e -> p (k e)"), ps, ACT.Copy).then_inc(s["act_tiles"], 1)
                elif kind == "uv":
                    act.wait_ge(s["consts"], CONSTS)
                    act.activation(uvT.rearrange("p k (h c) -> p (k h) c", c=32)[:, :, 0:D],
                                   ps.rearrange("p (h d) -> p h d", d=D), ACT.Copy).then_inc(s["act_tiles"], 1)
                elif kind == "wh":
                    act.activation(whT[:].rearrange("p k e -> p (k e)"), ps, ACT.Copy, scale=0.5
                                   ).then_inc(s["wh_split"], 1)
                    act.activation(wh_parts[:, 0].rearrange("p k e -> p (k e)"), ps, ACT.Copy, scale=0.5
                                   ).then_inc(s["act_tiles"], 1)
                elif kind in ("k", "q"):
                    tb, m, hf = where
                    i = SPLIT_OF[n]
                    c = m if kind == "q" else EC + m
                    scale = 0.25 if kind == "q" else 1.0
                    if i == 0:
                        act.wait_ge(s["b_scaled"], 3)
                    if i >= 2:
                        act.wait_ge(s["kq_mid"], i - 1)
                        act.wait_ge(s["kq_rest"], i - 1)
                        wait_stored(act, i - 2)
                    act.activation(full[:, i % 2], ps, ACT.Identity, bias=b_qk[:, c:c + 1], scale=scale
                                   ).then_inc(s["kq_hi"], 1)
                    act.activation(parts[:, i % 2, 0], ps, ACT.Identity, bias=b_qk[:, c:c + 1], scale=scale
                                   ).then_inc(s["kq_hi"], 1)
                    act.wait_ge(s["kq_hi"], 2 * (i + 1))
                    act.sem_inc(s["act_tiles"], 1)
                elif kind == "kimg":
                    for m in range(EC):
                        act.activation(img_full[:, m, :], ps[:, m * B:(m + 1) * B], ACT.Identity, bias=b_uk[:, m:m + 1]
                                       ).then_inc(s["img_hi"], 1)
                    for m in range(EC):
                        act.activation(parts_img[:, 0, m, :], ps[:, m * B:(m + 1) * B], ACT.Identity,
                                       bias=b_uk[:, m:m + 1]).then_inc(s["img_hi"], 1)
                    act.wait_ge(s["img_hi"], 2 * EC)
                    act.sem_inc(s["act_tiles"], 1)

            def weights(i, banks):
                qb = i // UNITS_0
                act.wait_ge(s["score_full"], i + 1)
                if i >= 2:
                    act.wait_ge(s["pv_full"], i - 1)
                for c in banks:
                    act.activation(prob[:, i % 2, c, :], pS[:, c if qb else i % 2, :], ACT.Exp
                                   ).then_inc(s["prob_ready"], 1)

            def image_weights(n):
                act.wait_ge(s["img_full_s"], n + 1)
                if n:
                    act.wait_ge(s["raw_ready"], G * n)
                act.activation(prob_img, pI[:], ACT.Exp).then_inc(s["img_prob"], 1)

            act.wait_ge(s["kq_mid"], len(SPLITS))
            act.wait_ge(s["kq_rest"], len(SPLITS))
            act.wait_ge(s["kq_low"], len(SPLITS))
            wait_stored(act, len(SPLITS) - 1)
            wait_stored(act, len(SPLITS) - 2)
            for i in range(FIRST):
                weights(i, range(i // UNITS_0 + 1))
                if i % G == 2:
                    image_weights(i // G)

            for t in range(S):
                g, st = t // GS, t % GS
                act.wait_ge(s["gate_sum"], t + 1)
                if t >= 2:
                    act.wait_ge(s["arg_ready"], t - 1)
                act.activation(gate[:, t % 2, :, 1], pG[:, g % 2, st * STEP:(st + 1) * STEP], ACT.Tanh
                               ).then_inc(s["gate_ready"], 1)
                act.wait_ge(s["arg_ready"], t + 1)
                if t >= 2:
                    act.wait_ge(s["h_low"], t - 1)
                act.activation(H1[:, t % 2], arg[:, t % 2, :, 1], ACT.Tanh).then_inc(s["h_hi"], 1)
                if st == 0:
                    if g >= 2:
                        act.wait_ge(s["y_ready"], EC * (g - 1))
                    else:
                        act.wait_ge(s["ones_q2"], 16)
                act.activation(Hf[:, t % (2 * GS), :], arg[:, t % 2, :, 1], ACT.Tanh).then_inc(s["h_full"], 1)
                if t < ATT_STEPS:
                    i, phase, n, ug = steps_of(t)
                    if phase in (1, 2):
                        weights(i, [phase - 1])
                    if phase == 3 and ug == 1:
                        image_weights(n)
                if 0 <= t - YT_FIRST < 4 * (B // 2) and (t - YT_FIRST) % 4 == 2:
                    rows_out = (t - YT_FIRST) // 4
                    act.wait_ge(s["yt_full"], rows_out + 1)
                    if rows_out >= 2:
                        act.wait_ge(s[f"out_sent{rows_out % 2}"], 16 * (rows_out // 2))
                    act.activation(y_out[:, rows_out % 2].rearrange("p b e -> p (b e)"), pS[:, rows_out % 2, :],
                                   ACT.Copy).then_inc(s["yt_copied"], 1)

        @block.vector
        def _(dve):
            dve.wait_ge(s["in_mask"], 16)
            dve.tensor_copy(mask_parts[:, 0, :], mask_in).then_inc(s["mask_p"], 1)
            dve.wait_ge(s["mask_p"], 1)
            dve.tensor_tensor(mask_rest, mask_in, mask_parts[:, 0, :], ALU.subtract).then_inc(s["mask_p"], 1)
            dve.wait_ge(s["mask_p"], 2)
            dve.tensor_copy(mask_parts[:, 1, :], mask_rest).then_inc(s["mask_p"], 1)
            dve.wait_ge(s["mask_p"], 3)
            dve.tensor_tensor(mask_parts[:, 2, :], mask_rest, mask_parts[:, 1, :], ALU.subtract
                              ).then_inc(s["mask_p"], 1)
            dve.wait_ge(s["bias_ready"], 1)
            dve.tensor_scalar(b_qk[:, 0:EC], b_qk[:, 0:EC], 0.25, None, ALU.mult).then_inc(s["b_scaled"], 1)
            dve.tensor_scalar(b_rec[:], b_rec[:], 0.5, None, ALU.mult).then_inc(s["b_scaled"], 1)
            dve.tensor_scalar(leak[:], alpha_in, -1.0, 1.0, ALU.mult, ALU.add).then_inc(s["b_scaled"], 1)

            def first_stage(n):
                kind, where, who = TILES[n]
                ps = bank(n)
                if kind in ("k", "q"):
                    i = SPLIT_OF[n]
                    dve.wait_ge(s["kq_hi"], 2 * (i + 1))
                    if i:
                        dve.wait_ge(s["kq_low"], i)
                    dve.tensor_tensor(rest, full[:, i % 2], parts[:, i % 2, 0], ALU.subtract
                                      ).then_inc(s["kq_rest"], 1)
                    dve.wait_ge(s["kq_mid"], i + 1)
                    dve.wait_ge(s["kq_rest"], i + 1)
                    dve.tensor_tensor(parts[:, i % 2, 2], rest, parts[:, i % 2, 1], ALU.subtract
                                      ).then_inc(s["kq_low"], 1)
                elif kind == "kimg":
                    dve.wait_ge(s["img_hi"], 2 * EC)
                    dve.tensor_tensor(img_rest[:], img_full[:], parts_img[:, 0], ALU.subtract
                                      ).then_inc(s["img_rest_s"], 1)
                    dve.wait_ge(s["img_rest_s"], 1)
                    dve.tensor_copy(parts_img[:, 1], img_rest[:]).then_inc(s["img_mid"], 1)
                    dve.wait_ge(s["img_mid"], 1)
                    dve.tensor_tensor(parts_img[:, 2], img_rest[:], parts_img[:, 1], ALU.subtract
                                      ).then_inc(s["img_low"], 1)
                elif kind == "v":
                    tb, b0 = where
                    dve.wait_ge(s["tile_full"], n + 1)
                    dve.wait_ge(s["consts"], CONSTS)
                    for i in range(2):
                        ins = dve.tensor_tensor(V[:, tb, b0 + i, :, 0:D],
                                                ps[:, i * E:(i + 1) * E].rearrange("p (h d) -> p h d", h=H),
                                                b_v[:].rearrange("p (h d) -> p h d", h=H), ALU.add)
                    ins.then_inc(s["dve_tiles"], 1)
                elif kind == "vimg":
                    dve.wait_ge(s["tile_full"], n + 1)
                    dve.tensor_copy(Vimg[:].rearrange("p g b -> p (g b)"), ps[:, 0:G * B]
                                    ).then_inc(s["dve_tiles"], 1)
                elif kind == "wh":
                    dve.wait_ge(s["act_tiles"], tiles_done("act", n))
                    dve.wait_ge(s["wh_split"], 1)
                    dve.wait_ge(s["mask_p"], 4)
                    w = [wh_parts[:, i].rearrange("p k e -> p (k e)") for i in range(3)]
                    dve.tensor_tensor(wh_rest[:], whT[:].rearrange("p k e -> p (k e)"), w[0], ALU.subtract
                                      ).then_inc(s["wh_split"], 1)
                    dve.wait_ge(s["wh_split"], 2)
                    dve.tensor_copy(w[1], wh_rest[:]).then_inc(s["wh_split"], 1)
                    dve.wait_ge(s["wh_split"], 3)
                    dve.tensor_tensor(w[2], wh_rest[:], w[1], ALU.subtract).then_inc(s["wh_split"], 3)

            def ring(n):
                kind, w = RING[n][:2]
                dve.wait_ge(s["ring_full"], n + 1)
                if kind == "max":
                    _, _, b, h0, nh = RING[n]
                    cols = 1 + P * (w // 2 + 1)
                    dve.tensor_reduce(row_max[:, w % 2].rearrange("p (h b) -> p h b", b=HALF)[:, h0:h0 + nh, b % HALF],
                                      pG[:, n % 2, 0:nh * cols].rearrange("p (h c) -> p h c", h=nh), AX_X, ALU.max
                                      ).then_inc(s["ring_read"], 1)
                    return
                k = 5 * w
                if w:
                    dve.wait_ge(s["shift_sent"], 48 * w)
                dve.tensor_scalar(shift[:], pG[0:H * HALF, n % 2, 0:P], -1.0, None, ALU.mult
                                  ).then_inc(s["ring_read"], 1)
                dve.wait_ge(s["ring_read"], n + 1)
                dve.tensor_copy(shift_parts[:, 0], shift[:]).then_inc(s["shift_step"], 2)
                dve.wait_ge(s["shift_step"], k + 2)
                dve.tensor_tensor(shift_rest[:], shift[:], shift_parts[:, 0], ALU.subtract
                                  ).then_inc(s["shift_step"], 1)
                dve.wait_ge(s["shift_step"], k + 3)
                dve.tensor_copy(shift_parts[:, 1], shift_rest[:]).then_inc(s["shift_step"], 1)
                dve.wait_ge(s["shift_step"], k + 4)
                dve.tensor_tensor(shift_parts[:, 2], shift_rest[:], shift_parts[:, 1], ALU.subtract
                                  ).then_inc(s["shift_step"], 1)

            def add_image(n, g):
                b = n % B
                if g == 0:
                    dve.wait_ge(s["pv_full"], G * (n + 1))
                    dve.wait_ge(s["img_prob"], n + 1)
                    if n:
                        dve.wait_ge(s["den_full"], n)
                        dve.wait_ge(s["att_ready"], G * n)
                c = slice(g * P, (g + 1) * P)
                dve.scalar_tensor_tensor(att_raw[:, c], prob_img[:, c], Vimg[:, g, b:b + 1], pV[:, c],
                                         ALU.mult, ALU.add).then_inc(s["raw_ready"], 1)

            def invert(n, first, count=1):
                if first == 0:
                    dve.wait_ge(s["den_full"], n + 1)
                c = slice(first * 64, (first + count) * 64)
                dve.reciprocal(att_inv[:, c], pX[:, c]).then_inc(s["inv_ready"], count)

            def divide(n, g):
                w = n // HALF
                dve.wait_ge(s["inv_ready"], 8 * n + 2 * (g + 1))
                if g == 0:
                    if w >= 2:
                        dve.wait_ge(s["proj_full"], EC * (w - 1))
                c = slice(g * P, (g + 1) * P)
                dve.tensor_tensor(att[:, w % 2, g, n % HALF, :], att_raw[:, c], att_inv[:, c], ALU.mult
                                  ).then_inc(s["att_ready"], 1)

            def add_x(w, m, i):
                qb, b0 = w // 2, (w % 2) * HALF + 2 * i
                dve.wait_ge(s["proj_full"], EC * w + m + 1)
                ps = pI if (w, m) == (QUARTERS - 1, 1) else pP
                z = zT[:, m, qb, b0:b0 + 2, :].rearrange("p b q -> p (b q)")
                dve.scalar_tensor_tensor(z, ps[:, 2 * i * P:2 * (i + 1) * P], b_proj[:, m:m + 1], z,
                                         ALU.add, ALU.add).then_inc(s["z_ready"], 1)

            for n in range(len(TILES_A)):
                first_stage(n)
            for n in range(len(TILES_B)):
                first_stage(len(TILES_A) + n)
                for r in ring_beside_tile(n):
                    ring(r)
            wait_stored(dve, len(SPLITS) - 1)
            wait_stored(dve, len(SPLITS) - 2)
            for i in range(FIRST):
                n, g = i // G, i % G
                for r in ring_beside_unit(i):
                    ring(r)
                if g == 0 and n:
                    for c in range(G):
                        add_image(n - 1, c)
                if g == 1 and n:
                    invert(n - 1, 0, 8)
                    for c in range(G):
                        divide(n - 1, c)
                if g == 3 and n % HALF == 0 and n:
                    for m in range(EC):
                        for c in range(2):
                            add_x(n // HALF - 1, m, c)

            def attention_piece(t, side):
                if t < ATT_STEPS:
                    i, phase, n, ug = steps_of(t)
                    for at, first in (((0, 3), 0), ((1, 0), 2)):
                        if (ug, phase) == at:
                            add_image(n - 1, first + side)
                    k = 4 * ug + phase - 8
                    if k >= 0 and side == 0:
                        invert(n - 1, k)
                    if k >= 0 and k % 2 == 1 and side == 1:
                        divide(n - 1, k // 2)
                k = t - ATT_STEPS
                if k in (2, 3):
                    add_image(BATCHES - 1, 2 * (k - 2) + side)
                if 5 <= k < 9:
                    invert(BATCHES - 1, 2 * (k - 5) + side)
                if 6 <= k < 10 and side == 0:
                    divide(BATCHES - 1, k - 6)
                if t in Z_AT and side == 1:
                    add_x(*Z_AT[t])

            dve.wait_ge(s["h0_ready"], 1)
            for t in range(S):
                g, st = t // GS, t % GS
                prev = (t + 2 * GS - 1) % (2 * GS)
                pair = zq[:, g % 2, st]
                if t:
                    dve.wait_ge(s["h_full"], t)
                    if t >= 2:
                        dve.wait_ge(s["gate_sum"], t)
                    dve.tensor_tensor(H2[:, (t - 1) % 2], Hf[:, prev, :], H1[:, (t - 1) % 2], ALU.subtract
                                      ).then_inc(s["h_low"], 1)
                if st == 0:
                    dve.wait_ge(s["zq_ready"], EC * (g + 1))
                for k in range(EC):
                    c = slice(k * B, (k + 1) * B)
                    dve.scalar_tensor_tensor(pair[:, c, 1], Hf[:, prev, c], leak[:, k:k + 1], pair[:, c, 0],
                                             ALU.mult, ALU.add).then_inc(s["q_ready"], 1)
                attention_piece(t, 0)
                dve.wait_ge(s["gate_ready"], t + 1)
                dve.wait_ge(s["q_ready"], EC * (t + 1))
                dve.tensor_tensor_scan(arg[:, t % 2].rearrange("p a b -> p (a b)"),
                                       gate[:, t % 2].rearrange("p a b -> p (a b)"),
                                       pair.rearrange("p a b -> p (a b)"), 0.0, ALU.mult, ALU.add
                                       ).then_inc(s["arg_ready"], 1)
                attention_piece(t, 1)

            for n in range(B // 2, BATCHES // 2):
                dve.wait_ge(s["yt_full"], n + 1)
                dve.wait_ge(s[f"out_sent{n % 2}"], 16 * (n // 2))
                dve.tensor_copy(y_out[:, n % 2].rearrange("p b e -> p (b e)"), pS[:, n % 2, :]
                                ).then_inc(s["yt_copied"], 1)


_INS = ["x", "cond_1024", "mask_Bx1x1xS_ff0", "L0_cond_c_attn_w", "L0_cond_c_attn_b", "L0_cond_c_proj_w",
        "L0_cond_c_proj_b", "L0_cond_uk_w", "L0_cond_uk_b", "L0_cond_uv_w", "L0_cond_uv_b", "L1_cond_W",
        "L1_cond_b", "L1_cond_alpha"]


def kernel(**inputs):
    import numpy as np
    import concourse.bacc as bacc
    from concourse.bass_utils import run_bass_kernel_spmd as run

    nc = bacc.Bacc("TRN2", target_bir_lowering=False, num_devices=1)
    arrays, args = {}, []
    for name in _INS:
        a = np.ascontiguousarray(inputs[name])
        arrays[f"in_{name}"] = a
        args.append(nc.dram_tensor(f"in_{name}", a.shape, mybir.dt.from_np(a.dtype), kind="ExternalInput").ap())
    out = nc.dram_tensor("out_0", (8, 256, 256), F32, kind="ExternalOutput").ap()
    build(nc, *args, out)
    r = run(nc, [arrays], core_ids=[0])
    return r.results[0]["out_0"]
```

```python
import concourse.bass as bass
from concourse import mybir
from contextlib import ExitStack

F32 = mybir.dt.float32
BF16 = mybir.dt.bfloat16
F16 = mybir.dt.float16
I32 = mybir.dt.int32
ALU = mybir.AluOpType
ACT = mybir.ActivationFunctionType
AX_X = mybir.AxisListType.X

P = 128
HIDDEN_SCORE = -30000.0

PAIRS = [(0, 0), (0, 1), (1, 0), (1, 1), (0, 2), (2, 0)]




def build(nc, x, cond, mask, attn_w, attn_b, proj_w, proj_b, uk_w, uk_b, uv_w, uv_b, rec_w, rec_b, alpha, out):
    B, S, E = x.shape
    H, D = 16, 16
    EC = E // P
    TB = S // P
    G = H // 4
    HALF = B // 2
    NQ = HALF * P
    SLOTS = len(PAIRS) * D
    MASK0, SHIFT0, ROWS = SLOTS, SLOTS + 3, SLOTS + 6
    STEP = EC * B
    GS = 16
    NG = S // GS
    KP = P + 1
    QUARTERS = TB * 2
    QT = S // QUARTERS
    DUOS = QUARTERS * HALF
    UNITS = DUOS * G
    UNITS_0 = UNITS // 2
    EARLY = 2
    FIRST = (HALF + EARLY) * G
    VD = D + 1

    ctx = ExitStack()
    with ctx:
        def sb(name, shape, dt=F32):
            return ctx.enter_context(nc.sbuf_tensor(name, shape, dt))

        def sem(name):
            return ctx.enter_context(nc.semaphore(name))

        def dram(name, shape, dt):
            return nc.dram_tensor(name, shape, dt, kind="Internal").ap()

        xin = sb("xin", [P, TB, B, E])
        region = sb("region", [P, 15 * NQ])

        def view(first, count, pattern=None, **sizes):
            v = region[:, first * NQ:(first + count) * NQ]
            return v.rearrange(pattern, **sizes) if pattern else v

        full = view(0, 2, "p (a n) -> p a n", a=2)
        rest = view(2, 1)
        w_attn = view(3, 3, "p (c e) -> p c e", c=EC)
        w_uk = view(6, 1, "p (c e) -> p c e", c=EC)
        w_uv = view(7, 1, "p (c e) -> p c e", c=EC)
        ukT = view(8, 1, "p (c e) -> p c e", c=EC)
        uvT = view(9, 2, "p (c n) -> p c n", c=EC)
        parts_flat = view(11, 4).bitcast(BF16)[:, 0:2 * 3 * HALF * KP].rearrange("p (a i n) -> p a i n", a=2, i=3)

        def parts_of(kind, a):
            if kind == "q":
                return parts_flat[:, a, :, 0:NQ]
            return parts_flat[:, a].rearrange("p i (b n) -> p i b n", n=KP)[:, :, :, 1:KP]

        def part_of(n, i):
            return parts_of(SPLITS[n][0], n % 2)[:, i]

        def full_of(n):
            v = full[:, n % 2]
            return v if SPLITS[n][0] == "q" else v.rearrange("p (b n) -> p b n", n=P)

        prob = view(0, 4, "p (a c n) -> p a c n", a=2, c=2)
        att = view(4, 8, "p (a g b q) -> p a g b q", a=2, g=G, b=HALF)
        att_raw = [view(12, 1), view(14, 1)]
        prob_img = view(13, 1)
        y_out = view(0, 2, "p (a b e) -> p a b e", a=2, b=2)
        w_proj = sb("w_proj", [P, G, E])
        w_rec = sb("w_rec", [P, EC, 2 * E])
        cond_in = sb("cond_in", [B, E])
        bias_rows = sb("bias_rows", [6 * EC, P])
        bias_cols = sb("bias_cols", [P, 6 * EC])
        b_qk, b_uk = bias_cols[:, 0:2 * EC], bias_cols[:, 2 * EC:3 * EC]
        b_proj, alpha_in = bias_cols[:, 3 * EC:4 * EC], bias_cols[:, 4 * EC:5 * EC]
        b_gate = bias_cols[:, 5 * EC:6 * EC]
        b_v = sb("b_v", [P, E])
        b_uv = sb("b_uv", [1, G * P])
        ident = sb("ident", [P, P])
        ident_b = sb("ident_b", [P, P], BF16)
        causal_qk = sb("causal_qk", [P, QT], BF16)
        causal_kq = sb("causal_kq", [P, P], BF16)
        ones_row = sb("ones_row", [1, P])
        den = sb("den", [P, 512 * 4 // P])
        den_inv = sb("den_inv", [P, 512 * 4 // P])

        xT = sb("xT", [P, EC, TB, B, P])
        zT = xT
        condT = sb("condT", [P, EC, B])
        parts_img = sb("parts_img", [P, 3, EC, B], BF16)
        img_full = sb("img_full", [P, EC, B])
        img_rest = sb("img_rest", [P, EC, B])
        mask_parts = sb("mask_parts", [B, 3, TB, KP], BF16)
        Kst = sb("Kst", [P, TB, H, B * KP], BF16)
        Qst = sb("Qst", [P, 2, H, NQ], BF16)
        Qbuf = [Qst[:, 0], Qst[:, 1], xin[:].rearrange("p t b e -> p (t b e)").bitcast(BF16).rearrange(
            "p (h n) -> p h n", h=H)]
        Kimg = sb("Kimg", [P, H, B], BF16)
        Vimg = sb("Vimg", [P, G, B])
        Vflat = sb("V", [P, TB * B * H * VD + 32 - VD])
        V = Vflat[:, 0:TB * B * H * VD].rearrange("p (t b h d) -> p t b h d", t=TB, b=B, h=H)
        row_max = sb("row_max", [P, 2, H * HALF])
        shift = sb("shift", [H * HALF, P])
        shift_rest = sb("shift_rest", [H * HALF, P])
        shift_parts = sb("shift_parts", [H * HALF, 3, P], BF16)

        whT = sb("whT", [P, EC, E])
        wzT = sb("wzT", [P, EC, E])
        att_inv = sb("att_inv", [P, 512])
        mask_in, mask_rest = att_inv[0:B, 0:S], att_inv[0:B, S:2 * S]
        wh_parts = sb("wh_parts", [P, 2, EC, E], F16)
        tops = sb("tops", [P, EC])
        row_top = sb("row_top", [P, 1])
        row_scale = sb("row_scale", [P, 1])
        gate_scale = sb("gate_scale", [P, 1])
        b_gate_parts = sb("b_gate_parts", [P, 3, EC])
        b_gate_rest = sb("b_gate_rest", [P, EC])
        b_gate_hi = sb("b_gate_hi", [P, 3, EC], BF16)
        b_gate_rows = sb("b_gate_rows", [3 * EC, P], BF16)
        sel_gate = sb("sel_gate", [3 * EC, GS * STEP], BF16)
        leak = sb("leak", [P, EC])
        zq = w_rec[:].rearrange("p c e -> p (c e)").rearrange("p (a t c i) -> p a t c i", a=2, t=GS, i=2)
        Hf = sb("Hf", [P, 2 * GS, STEP])
        ones_rows = Hf[0:3, 0:GS].rearrange("p t c -> p (t c)").bitcast(BF16)
        H1 = sb("H1", [P, 2, STEP], F16)
        H2 = sb("H2", [P, 2, STEP], F16)
        gate = sb("gate", [P, 2, STEP, 2])

        def psum(name, shape):
            return ctx.enter_context(nc.psum_tensor(name, shape, F32))

        pG = psum("pG", [P, 2, 512])
        pS = psum("pS", [P, 2, 512])
        pP = psum("pP", [P, 512])
        pI = psum("pI", [P, 512])
        pV = psum("pV", [P, 512])
        pA = psum("pA", [P, 512])
        arg = pA[:, 0:4 * STEP].rearrange("p (a c i) -> p a c i", a=2, i=2)

        scr = {"k": dram("scr_k", [3, E, TB, B * KP], BF16), "q": dram("scr_q", [3, E, TB, B * P], BF16)}
        scr_img = dram("scr_img", [3, E, B], BF16)
        scr_den = dram("scr_den", [2, 4, 512], F32)
        scr_inv = dram("scr_inv", [2, 4, 512], F32)
        scr_mask = dram("scr_mask", [3, TB, B * KP], BF16)

        names = """in_x0a in_x0b in_x1 in_cond
            in_uk in_attn_k in_attn_q in_attn_v in_bias in_v_bias in_uv in_rec in_mask in_proj consts
            tile_full act_tiles dve_tiles kq_hi kq_mid kq_rest kq_low kq_stored0 kq_stored1
            img_hi img_rest_s img_mid img_low img_stored img_stacked img_placed
            mask_p mask_stored mask_stacked ones_k ones_q ones_q2
            stack_k0 stack_k1 stack_k2 stack_k3 stack_q0 stack_q1 stack_q2 stack_q3
            ring_full ring_read shift_step shift_sent last_shift_sent
            score_full prob_ready pv_full img_full_s img_prob raw_ready den_stored den_sent den_inverted
            inv_stored inv_spread att_ready proj_full z_ready wh_split bias_ready b_scaled h0_ready top_step
            b_step w_scaled zq_ready y_ready seeded gate_sum gate_ready h_hi h_full h_low
            q_ready arg_ready yt_full yt_copied out_sent0 out_sent1""".split()
        s = {n: sem(n) for n in names}
        CONSTS = 24

        block = ctx.enter_context(nc.Block())

        def x_tiles(tb):
            return [("x", (tb, k, hf), "act") for hf in range(2) for k in range(EC)]

        def kq_tiles(kind, tb):
            return [(kind, (tb, m, hf), "act") for hf in range(2) for m in range(EC)]

        def v_tiles(tb):
            return [("v", (tb, b), "dve") for b in range(0, B, 2)]

        TILES_A = (x_tiles(0) + [("cond", (), "act")] + kq_tiles("k", 0) + kq_tiles("q", 0)
                   + [("uk", (), "act"), ("kimg", (), "act"), ("uv", (), "act"), ("vimg", (), "dve")]
                   + v_tiles(0) + x_tiles(1))
        TILES_B = (kq_tiles("k", 1) + kq_tiles("q", 1) + v_tiles(1)
                   + [("wh", (), "act"), ("wz", (), "act"), ("bg", (), "act")])
        TILES = TILES_A + TILES_B
        BANKS = 4

        def bank(n):
            return [pS[:, 0, :], pS[:, 1, :], pP[:], pI[:]][n % BANKS]

        def tiles_done(engine, n):
            return sum(t[2] == engine for t in TILES[:n + 1])

        def wait_tile_empty(eng, n):
            who = TILES[n][2]
            eng.wait_ge(s[f"{who}_tiles"], tiles_done(who, n))

        def tile_at(kind, where=None):
            return next(n for n, t in enumerate(TILES) if t[0] == kind and (where is None or t[1] == where))

        SPLITS = [t for t in TILES if t[0] in "kq"]
        SPLIT_OF = {n: i for i, n in enumerate(n for n, t in enumerate(TILES) if t[0] in "kq")}

        def wait_stored(eng, n):
            eng.wait_ge(s[f"kq_stored{n % 2}"], 16 * (n // 2 + 1))

        RING = []
        for w in range(QUARTERS):
            nh = (4, 2, 2, 1)[w]
            RING += [("max", w, duo, h, nh) for duo in range(HALF) for h in range(0, H, nh)]
            RING.append(("turn", w))

        def keys_seen(w):
            return QT * (w % 2 + 1)

        def ring_at(w):
            return RING.index(("turn", w))

        def ring_beside_tile(n):
            share = 3
            return range(min(n * share, ring_at(0) + 1), min((n + 1) * share, ring_at(0) + 1))

        def ring_beside_unit(i):
            for w, first, units in ((1, 0, 10), (2, 10, 10)):
                lo, hi = ring_at(w - 1) + 1, ring_at(w) + 1
                share = -(-(hi - lo) // units)
                if first <= i < first + units:
                    return range(min(lo + (i - first) * share, hi), min(lo + (i - first + 1) * share, hi))
            return range(0)

        def probs_done(i):
            return i + 1 + max(0, i + 1 - UNITS_0)

        def starts(i):
            return 3 * (min(i, UNITS_0) - FIRST) + 4 * max(0, i - UNITS_0)

        def at_step(t):
            i = max(i for i in range(FIRST, UNITS + 4 * G) if starts(i) <= t)
            return i, t - starts(i), starts(i + 1) == t + 1, i // G, i % G

        def inverted_at(m):
            return starts((m + 1) * G + 2) + 2

        DIVIDE_AT = {inverted_at(m) + 7 + k: (m, k) for m in range(FIRST // G - 2, DUOS) for k in range(2)}
        PROJ_AT = {}
        for w in range(1, QUARTERS):
            first = inverted_at(HALF * (w + 1) - 1) + 9
            offsets = range(EC * G) if w == QUARTERS - 1 else (0, 1, 4, 5, 7, 8, 9, 10)
            PROJ_AT |= {first + offsets[p]: (w, p) for p in range(EC * G)}
        Z_AT = {}
        for t_, (w_, p_) in PROJ_AT.items():
            if p_ % G == G - 1:
                Z_AT |= {(t_ + 1, 1): (w_, p_ // G, 0), (t_ + 2, 0): (w_, p_ // G, 1)}
        RING_LATE = ring_at(2) + 1
        second_proj = min(t for t, (w, _) in PROJ_AT.items() if w == 1)
        second_z = max(t for (t, _), (w, _, _) in Z_AT.items() if w == 1)
        late_steps = [t for t in range(1, S) if t < second_proj - 1 or t > second_z + 1]
        RING_AT = dict(zip(late_steps, range(RING_LATE, len(RING))))
        RING_BEFORE_SECOND = 1 + max(r for t, r in RING_AT.items() if t < second_proj)

        def projection_bank(w, m):
            return {(0, 1): pA, (QUARTERS - 1, 1): pI}.get((w, m), pP)

        def ring_bank(n):
            return pG[:, n % 2, :] if n < RING_LATE else pP[:]

        SEED_AT = {11: (0, 1, 2), 15: (3, 4)}
        YT_FIRST = S - 64

        assert max(RING_AT) + 4 < starts(3 * HALF * G)

        def store_shift(eng, w):
            for i in range(3):
                eng.dma_start(Qbuf[w % 3][SHIFT0 + i:SHIFT0 + i + 1].rearrange("o h (b q) -> o (h b) q", b=HALF),
                              shift_parts[:, i, :]
                              ).then_inc(s["shift_sent" if w < QUARTERS - 1 else "last_shift_sent"], 16)

        @block.sync
        def _(sp):
            def rows_of(b0, b1, tb):
                return x[b0:b1, tb * P:(tb + 1) * P, :].rearrange("b p e -> p b e")
            sp.dma_start(xin[:, 0, 0:HALF], rows_of(0, HALF, 0)).then_inc(s["in_x0a"], 16)
            w_in = attn_w.rearrange("(c p) e -> p c e", p=P)
            sp.dma_start(w_attn[:, :, E:2 * E], w_in[:, :, E:2 * E]).then_inc(s["in_attn_k"], 16)
            for row, vec in ((0, attn_b[0:2 * E]), (2 * EC, uk_b), (3 * EC, proj_b), (4 * EC, alpha),
                             (5 * EC, rec_b)):
                rows = vec.rearrange("(m p) -> m p", p=P)
                sp.dma_start(bias_rows[row:row + rows.shape[0]], rows).then_inc(s["in_bias"], 16)
            sp.dma_start(cond_in[:], cond).then_inc(s["in_cond"], 16)
            sp.dma_start(xin[:, 0, HALF:B], rows_of(HALF, B, 0)).then_inc(s["in_x0b"], 16)
            sp.dma_start(w_attn[:, :, 0:E], w_in[:, :, 0:E]).then_inc(s["in_attn_q"], 16)
            sp.dma_start(w_attn[:, :, 2 * E:3 * E], w_in[:, :, 2 * E:3 * E]).then_inc(s["in_attn_v"], 16)
            sp.dma_start(b_v[:], attn_b[2 * E:3 * E].rearrange("(a e) -> a e", a=1).to_broadcast([P, E])
                         ).then_inc(s["in_v_bias"], 16)
            sp.dma_start(mask_in, mask.rearrange("b i j k -> (b i j) k")).then_inc(s["in_mask"], 16)
            sp.dma_start(w_uk, uk_w.rearrange("(c p) e -> p c e", p=P)).then_inc(s["in_uk"], 16)
            sp.wait_ge(s["consts"], CONSTS)
            sp.dma_start(b_uv[:].rearrange("a (h c) -> a h c", c=32)[:, :, 0:D],
                         uv_b.rearrange("(a h d) -> a h d", a=1, d=D)).then_inc(s["in_v_bias"], 16)
            sp.dma_start(w_uv, uv_w.rearrange("(c p) e -> p c e", p=P)).then_inc(s["in_uv"], 16)

            def ones(dst, name):
                src = ones_rows[:, None, 0:dst.shape[2]]
                sp.dma_start(dst, src.to_broadcast(list(dst.shape))).then_inc(s[name], 16)

            ones_n = 2 * GS * STEP
            def store_split(n):
                kind, (tb, m, hf), _ = SPLITS[n]
                sp.wait_ge(s["kq_hi"], 2 * (n + 1))
                sp.wait_ge(s["kq_mid"], n + 1)
                sp.wait_ge(s["kq_low"], n + 1)
                width = NQ if kind == "q" else HALF * KP
                to = scr[kind][:, m * P:(m + 1) * P, tb, hf * width:(hf + 1) * width]
                sp.dma_start(to.rearrange("i p n -> p i n"), parts_flat[:, n % 2, :, 0:width]).then_inc(s[f"kq_stored{n % 2}"], 16)

            def stack(kind, tb, hf, pairs=range(len(PAIRS))):
                w = 2 * tb + hf
                last = max(n for n, t in enumerate(SPLITS) if t[0] == kind and t[1][0] == tb and t[1][2] == hf)
                wait_stored(sp, last)
                wait_stored(sp, last - 1)
                width = NQ if kind == "q" else HALF * KP
                cols = slice(hf * width, (hf + 1) * width)
                for i in pairs:
                    pq, pk = PAIRS[i]
                    src = scr[kind][pk if kind == "k" else pq, :, tb, cols].rearrange("(h d) n -> d h n", d=D)
                    to = slice(i * D, (i + 1) * D)
                    dst = Kst[to, tb, :, cols] if kind == "k" else Qbuf[w % 3][to]
                    sp.dma_start(dst, src).then_inc(s[f"stack_{kind}{w}"], 16)

            for n in range(4):
                store_split(n)
            sp.dma_start(xin[:, 1], rows_of(0, B, 1)).then_inc(s["in_x1"], 16)
            for n in range(4, 8):
                stack("k", 0, (n - 4) // 2, range(3 * (n % 2), 3 * (n % 2) + 3))
                store_split(n)
            ones(Kst[SHIFT0:SHIFT0 + 3].rearrange("i t h (c n) -> i (t h c) n", n=HALF * KP // 2), "ones_k")
            ones(Qst[MASK0:MASK0 + 3].rearrange("i a h (c n) -> i (a h c) n", n=ones_n), "ones_q")
            stack("q", 0, 0)
            sp.wait_ge(s["mask_p"], 4)
            for i in range(3):
                sp.dma_start(scr_mask[i].rearrange("t (b q) -> b t q", b=B),
                             mask_parts[:, i]).then_inc(s["mask_stored"], 16)
            sp.wait_ge(s["img_low"], 1)
            for m in range(EC):
                sp.dma_start(scr_img[:, m * P:(m + 1) * P, :].rearrange("i p b -> p i b"), parts_img[:, :, m, :]
                             ).then_inc(s["img_stored"], 16)
            sp.wait_ge(s["mask_stored"], 48)
            for tb in range(TB):
                sp.dma_start(Kst[MASK0:MASK0 + 3, tb], scr_mask[:, tb][:, None, :].to_broadcast([3, H, B * KP])
                             ).then_inc(s["mask_stacked"], 16)
            sp.wait_ge(s["img_stored"], 16 * EC)
            for i, (pq, pk) in enumerate(PAIRS):
                sp.dma_start(Kimg[i * D:(i + 1) * D], scr_img[pk].rearrange("(h d) b -> d h b", d=D)
                             ).then_inc(s["img_stacked"], 16)
            stack("q", 0, 1)
            for j in range(4):
                sp.dma_start(w_proj[32 * j:32 * j + D], proj_w.rearrange("(g j d) n -> j d g n", g=G, j=4)[j]
                             ).then_inc(s["in_proj"], 16)
            sp.dma_start(w_rec[:], rec_w.rearrange("(c p) e -> p c e", p=P)).then_inc(s["in_rec"], 16)
            for n in range(8, 11):
                store_split(n)
            wait_tile_empty(sp, tile_at("x", (1, EC - 1, 1)))
            ones(Qbuf[2][MASK0:MASK0 + 3].rearrange("i h (c n) -> i (h c) n", n=ones_n), "ones_q2")
            store_split(11)
            stack("k", 1, 0)
            store_split(12)
            store_split(13)
            stack("k", 1, 1)
            store_split(14)
            store_split(15)
            stack("q", 1, 0)
            for n in range(DUOS):
                if n == HALF - 1:
                    sp.wait_ge(s["score_full"], UNITS_0 // 2)
                    sp.wait_ge(s["img_full_s"], HALF)
                    stack("q", 1, 1)
                sp.wait_ge(s["raw_ready"], G * (n + 1))
                sp.dma_start(scr_den[n % 2], att_raw[n % 2][D:P:32]).then_inc(s["den_stored"], 16)
                sp.wait_ge(s["den_stored"], 16 * (n + 1))
                sp.dma_start(den[:], scr_den[n % 2].rearrange("j (p c) -> (j p) c", p=32)).then_inc(s["den_sent"], 16)
                if n == DUOS - HALF - 2:
                    sp.wait_ge(s["shift_step"], 5 * QUARTERS)
                    store_shift(sp, QUARTERS - 1)
                sp.wait_ge(s["den_inverted"], n + 1)
                sp.dma_start(scr_inv[n % 2].rearrange("j (p c) -> (j p) c", p=32), den_inv[:]
                             ).then_inc(s["inv_stored"], 16)
                sp.wait_ge(s["inv_stored"], 16 * (n + 1))
                if n:
                    sp.wait_ge(s["att_ready"], G * n)
                for j in range(4):
                    sp.dma_start(att_inv[32 * j:32 * (j + 1)], scr_inv[n % 2, j:j + 1].to_broadcast([32, 512])
                                 ).then_inc(s["inv_spread"], 16)

            for n in range(DUOS // 2):
                tb, b = n // (B // 2), 2 * (n % (B // 2))
                sp.wait_ge(s["yt_copied"], n + 1)
                sp.dma_start(out[b:b + 2, tb * P:(tb + 1) * P, :].rearrange("b p e -> p b e"),
                             y_out[:, n % 2]).then_inc(s[f"out_sent{n % 2}"], 16)
            for half in range(2):
                sp.wait_ge(s[f"out_sent{half}"], 16 * (DUOS // 4))

        @block.gpsimd
        def _(pool):
            n = 0

            def step(ins):
                ins.then_inc(s["consts"], 1)
                pool.wait_ge(s["consts"], n + 1)
                return 1
            n += step(pool.memset(ident[:], 0.0))
            n += step(pool.affine_select(out=ident[:], in_=ident[:], compare_op=ALU.not_equal, fill=1.0, base=0,
                                         pattern=[[-1, P]], channel_multiplier=1))
            n += step(pool.memset(b_uv[:], 1.0))
            n += step(pool.memset(uvT, 0.0))
            n += step(pool.memset(ones_rows, 1.0))
            n += step(pool.memset(w_proj[:], 0.0))
            n += step(pool.memset(Vflat[:], 1.0))
            n += step(pool.memset(ones_row[:], 1.0))
            n += step(pool.memset(sel_gate[:], 0.0))
            for i in range(3):
                n += step(pool.affine_select(out=sel_gate[:].rearrange("k (t m b) -> k t m b", t=GS, m=EC),
                                             in_=sel_gate[:].rearrange("k (t m b) -> k t m b", t=GS, m=EC),
                                             compare_op=ALU.not_equal, fill=1.0, base=-EC * i,
                                             pattern=[[0, GS], [-1, EC], [0, B]], channel_multiplier=1))
            n += step(pool.tensor_copy(ident_b[:], ident[:]))
            n += step(pool.memset(causal_qk[:], 0.0))
            for e in range(2):
                own = causal_qk[e * QT:(e + 1) * QT]
                n += step(pool.affine_select(out=own, in_=own, compare_op=ALU.is_ge,
                                             fill=HIDDEN_SCORE, base=0, pattern=[[-1, QT]], channel_multiplier=1))
            n += step(pool.memset(causal_kq[:], 0.0))
            n += step(pool.affine_select(out=causal_kq[:], in_=causal_kq[:], compare_op=ALU.is_ge,
                                         fill=HIDDEN_SCORE, base=0, pattern=[[1, P]], channel_multiplier=-1))
            n += step(pool.memset(Kimg[SLOTS:P], 1.0))
            n += step(pool.affine_select(out=Kimg[SLOTS:P], in_=Kimg[SLOTS:P], compare_op=ALU.is_ge, fill=0.0,
                                         base=-(SHIFT0 - SLOTS), pattern=[[0, H], [0, B]], channel_multiplier=1))
            n += step(pool.memset(gate[:], 0.0))
            n += step(pool.memset(mask_parts[:], 0.0))
            n += step(pool.memset(parts_flat.rearrange("p a i (b n) -> p (a i b) n", n=KP)[:, :, 0:1], 0.0))
            n += step(pool.memset(H1[:, 1], 0.0))
            assert n == CONSTS

            for i in range(len(SPLITS)):
                pool.wait_ge(s["kq_hi"], 2 * (i + 1))
                if i >= 2:
                    wait_stored(pool, i - 2)
                pool.tensor_tensor(part_of(i, 1), full_of(i), part_of(i, 0), ALU.subtract
                                   ).then_inc(s["kq_mid"], 1)

            for w in range(QUARTERS - 1):
                pool.wait_ge(s["shift_step"], 5 * (w + 1))
                store_shift(pool, w)

            def halve(g):
                tb, q0 = (g * GS) // P, (g * GS) % P
                if g >= 2:
                    pool.wait_ge(s["arg_ready"], GS * (g - 1))
                    pool.wait_ge(s["seeded"], 5 * (g - 1))
                pool.wait_ge(s["z_ready"], 2 * EC * (g * GS // QT + 1))
                for k in range(EC):
                    src = zT[:, k, tb, :, q0:q0 + GS].rearrange("p b q -> p q b")
                    pool.tensor_scalar(zq[:, g % 2, :, k * B:(k + 1) * B, 0], src, 0.5, None, ALU.mult
                                       ).then_inc(s["zq_ready"], 1)

            def add_z(g):
                tb, q0 = (g * GS) // P, (g * GS) % P
                pool.wait_ge(s["h_full"], GS * (g + 1))
                pool.wait_ge(s["zq_ready"], EC * (g + 1))
                for k in range(EC):
                    z = zT[:, k, tb, :, q0:q0 + GS].rearrange("p b q -> p q b")
                    h = Hf[:, (g % 2) * GS:(g % 2 + 1) * GS, k * B:(k + 1) * B]
                    pool.tensor_tensor(z, z, h, ALU.add).then_inc(s["y_ready"], 1)

            halve(0)
            halve(1)
            for g in range(NG):
                if g + 2 < NG:
                    pool.wait_ge(s["h_full"], GS * (g + 1))
                    halve(g + 2)
                add_z(g)

        @block.tensor
        def _(pe):
            pe.wait_ge(s["consts"], 2)
            seen = set()

            def wait_once(name, value=16):
                if (name, value) not in seen:
                    seen.add((name, value))
                    pe.wait_ge(s[name], value)

            def first_stage(n):
                kind, where, who = TILES[n]
                if n >= BANKS:
                    wait_tile_empty(pe, n - BANKS)
                ps = bank(n)
                if kind == "x":
                    tb, k, hf = where
                    wait_once("in_x1" if tb else "in_x0" + "ab"[hf])
                    for i in range(HALF):
                        last = pe.transpose(ps[:, i * P:(i + 1) * P], xin[:, tb, hf * HALF + i, k * P:(k + 1) * P],
                                            ident[:])
                elif kind == "cond":
                    wait_once("in_cond")
                    wait_once("in_bias", 16 * 5)
                    pe.transpose(ps[:, STEP:STEP + 6 * EC], bias_rows[:], ident[0:6 * EC, 0:6 * EC])
                    for k in range(EC):
                        last = pe.transpose(ps[:, k * B:(k + 1) * B], cond_in[:, k * P:(k + 1) * P], ident[0:B, 0:B])
                elif kind in ("uk", "uv", "wh", "wz"):
                    if kind[0] == "w":
                        wait_once("w_scaled", EC + 1)
                    else:
                        wait_once("in_" + kind)
                    w, o = {"uk": (w_uk, 0), "uv": (w_uv, 0), "wh": (w_rec, 0), "wz": (w_rec, E)}[kind]
                    for k in range(EC):
                        for m in range(EC):
                            last = pe.transpose(ps[:, k * E + m * P:k * E + (m + 1) * P],
                                                w[:, m, o + k * P:o + (k + 1) * P], ident[:])
                elif kind == "bg":
                    last = pe.transpose(ps[0:3 * EC, 0:P], b_gate_parts[:].rearrange("p i m -> p (i m)"), ident[:])
                elif kind in ("k", "q"):
                    tb, m, hf = where
                    wait_once("in_attn_" + kind)
                    wait_tile_empty(pe, tile_at("x", (tb, EC - 1, hf if kind == "k" else 1)))
                    o = (0 if kind == "q" else E) + m * P
                    for k in range(EC):
                        if kind == "k":
                            cols = xT[:, k, tb, hf * HALF:(hf + 1) * HALF, :].rearrange("p b q -> p (b q)")
                            to = ps
                        else:
                            cols = xT[:, k, tb, :, hf * QT:(hf + 1) * QT]
                            to = ps.rearrange("p (b q) -> p b q", b=B)
                        last = pe.matmul(to, w_attn[:, k, o:o + P], cols, start=(k == 0), stop=(k == EC - 1))
                elif kind == "kimg":
                    wait_tile_empty(pe, tile_at("uk"))
                    for m in range(EC):
                        for k in range(EC):
                            last = pe.matmul(ps[:, m * B:(m + 1) * B], ukT[:, k, m * P:(m + 1) * P], condT[:, k, :],
                                             start=(k == 0), stop=(k == EC - 1), skip_group_check=True)
                elif kind == "v":
                    tb, b0 = where
                    wait_once("in_attn_v")
                    wait_once("in_v_bias", 16 * 2)
                    for i in range(2):
                        for k in range(EC):
                            last = pe.matmul(ps[:, i * E:(i + 1) * E], xT[:, k, tb, b0 + i, :],
                                             w_attn[:, k, 2 * E:3 * E], start=(k == 0), stop=(k == EC - 1),
                                             skip_group_check=True)
                elif kind == "vimg":
                    wait_tile_empty(pe, tile_at("uv"))
                    wait_once("consts", CONSTS)
                    wait_once("in_v_bias", 16 * 2)
                    for g in range(G):
                        dst = ps[:, g * B:(g + 1) * B]
                        pe.matmul(dst, b_uv[:, g * P:(g + 1) * P], ones_row[:, 0:B], start=True, stop=False,
                                  skip_group_check=True)
                        for k in range(EC):
                            last = pe.matmul(dst, uvT[:, k, g * P:(g + 1) * P], condT[:, k, :],
                                             start=False, stop=(k == EC - 1), skip_group_check=True)
                last.then_inc(s["tile_full"], 1)

            def ring(n):
                kind, w = RING[n][:2]
                qb = w // 2
                ps = ring_bank(n)
                if kind == "turn":
                    pe.wait_ge(s["ring_read"], n)
                    pe.transpose(ps[0:H * HALF, 0:P], row_max[:, w % 2, :], ident[:]).then_inc(s["ring_full"], 1)
                    return
                _, _, duo, h0, nh = RING[n]
                wait_once(f"stack_k{2 * qb}", 96)
                wait_once(f"stack_k{2 * qb + 1}", 96)
                wait_once(f"stack_q{w}", 96)
                if n >= RING_LATE:
                    pe.wait_ge(s["ring_read"], n)
                    pe.wait_ge(s["z_ready"], 2 * EC * (1 if n < RING_BEFORE_SECOND else 2))
                elif n >= 2:
                    pe.wait_ge(s["ring_read"], n - 1)
                cols = 1 + P * qb + keys_seen(w)
                for j in range(nh):
                    h, c0 = h0 + j, j * cols
                    for e in range(2):
                        b = 2 * duo + e
                        rows = slice(e * QT, (e + 1) * QT)
                        lhs = Qbuf[w % 3][:, h, b * QT:(b + 1) * QT]
                        for c in range(qb + 1):
                            nk = keys_seen(w) if c == qb else P
                            k0, k1 = b * KP + (c > 0), b * KP + 1 + nk
                            to = c0 + c * KP
                            pe.matmul(ps[rows, to:to + k1 - k0], lhs[0:SHIFT0], Kst[0:SHIFT0, c, h, k0:k1],
                                      start=True, stop=(c < qb), skip_group_check=True)
                    last = pe.matmul(ps[:, c0 + cols - QT:c0 + cols], ident_b[:], causal_qk[:], start=False, stop=True,
                                     skip_group_check=True)
                last.then_inc(s["ring_full"], 1)

            def queries(n, h, e):
                w, b = n // HALF, 2 * (n % HALF) + e
                return Qbuf[w % 3][0:ROWS, h, b * QT:(b + 1) * QT]

            def wait_shift(w):
                if w < QUARTERS - 1:
                    wait_once("shift_sent", 48 * (w + 1))
                else:
                    wait_once("last_shift_sent", 48)

            def image_scores(n, heads=range(H)):
                if heads[0] == 0:
                    if n:
                        pe.wait_ge(s["img_prob"], n)
                    wait_shift(n // HALF)
                for h in heads:
                    j, g = h % 4, h // 4
                    for e in range(2):
                        b, c = 2 * (n % HALF) + e, g * P + e * QT
                        last = pe.matmul(pI[32 * j:32 * j + 32, c:c + QT],
                                         Kimg[0:ROWS, h, b:b + 1].to_broadcast([ROWS, 32]), queries(n, h, e),
                                         start=True, stop=True, skip_group_check=True)
                if heads[-1] == H - 1:
                    last.then_inc(s["img_full_s"], 1)

            def scores(i):
                n, g = i // G, i % G
                w = n // HALF
                qb = w // 2
                if i >= 2:
                    pe.wait_ge(s["prob_ready"], probs_done(i - 1 if qb else i - 2))
                wait_shift(w)
                own = 0 if qb else i % 2
                hidden = causal_kq[:, None, (w % 2) * QT:(w % 2 + 1) * QT]
                pe.matmul(pS[:, own, :], ident_b[:], hidden.to_broadcast([P, 8, QT]),
                          start=True, stop=False, skip_group_check=True)
                for j in range(4):
                    h = 4 * g + j
                    for e in range(2):
                        b, c = 2 * (n % HALF) + e, j * P + e * QT
                        last = pe.matmul(pS[:, own, c:c + QT], Kst[0:ROWS, qb, h, b * KP + 1:(b + 1) * KP],
                                         queries(n, h, e), start=False, stop=True, skip_group_check=True)
                        if qb:
                            last = pe.matmul(pS[:, 1, c:c + QT], Kst[0:ROWS, 0, h, b * KP + 1:(b + 1) * KP],
                                             queries(n, h, e), start=True, stop=True, skip_group_check=True)
                last.then_inc(s["score_full"], 1)

            def values(i, heads=range(4)):
                n, g = i // G, i % G
                qb = n // HALF // 2
                if heads[0] == 0:
                    if g == 0 and n:
                        pe.wait_ge(s["raw_ready"], G * n)
                    pe.wait_ge(s["prob_ready"], probs_done(i))
                for j in heads:
                    for e in range(2):
                        b, to = 2 * (n % HALF) + e, g * P + e * QT
                        for c in range(qb + 1):
                            first = (((qb if c == 0 else 0) * B + b) * H + 4 * g + j) * VD
                            last = pe.matmul(pV[32 * j:32 * j + 32, to:to + QT], Vflat[:, first:first + 32],
                                             prob[:, i % 2, c, j * P + e * QT:j * P + (e + 1) * QT],
                                             start=(c == 0), stop=(c == qb), skip_group_check=True)
                if heads[-1] == 3:
                    last.then_inc(s["pv_full"], 1)

            def projection(w, p):
                m, g = p // G, p % G
                ps = projection_bank(w, m)
                if p == 0:
                    pe.wait_ge(s["att_ready"], G * HALF * (w + 1))
                if g == 0:
                    if (w, m) == (QUARTERS - 1, 1):
                        pe.wait_ge(s["img_prob"], DUOS)
                    elif w:
                        pe.wait_ge(s["ring_read"], RING_BEFORE_SECOND if w == 1 else len(RING))
                        pe.wait_ge(s["z_ready"], 2 * (EC * w + m))
                ins = pe.matmul(ps[:], w_proj[:, g, m * P:(m + 1) * P],
                                att[:, w % 2, g, :, :].rearrange("p b q -> p (b q)"),
                                start=(g == 0), stop=(g == G - 1))
                if g == G - 1:
                    ins.then_inc(s["proj_full"], 1)

            for n in range(len(TILES_A)):
                first_stage(n)
            wait_once("ones_k")
            wait_once("ones_q")
            wait_once("mask_stacked", 16 * TB)
            wait_once("img_placed", 1)
            for n in range(len(TILES_B)):
                first_stage(len(TILES_A) + n)
                for r in ring_beside_tile(n):
                    ring(r)
            pe.wait_ge(s["act_tiles"], tiles_done("act", len(TILES)))
            pe.wait_ge(s["dve_tiles"], tiles_done("dve", len(TILES)))
            wait_once("in_proj", 64)
            wait_once("ones_q2")

            def seed(g, i):
                dst = pG[:, g % 2, 0:GS * STEP].rearrange("p (t m b) -> p m t b", t=GS, m=EC)
                if i == 0:
                    pe.wait_ge(s["zq_ready"], EC * (g + 1))
                if i == 0:
                    ins = pe.matmul(pG[:, g % 2, 0:GS * STEP], b_gate_rows[:], sel_gate[:], start=True, stop=False,
                                    skip_group_check=True)
                else:
                    k, m = (i - 1) // 2, (i - 1) % 2
                    ins = pe.matmul(dst[:, m], wzT[:, k, m * P:(m + 1) * P], zq[:, g % 2, :, k * B:(k + 1) * B, 0],
                                    start=False, stop=True, skip_group_check=True)
                ins.then_inc(s["seeded"], 1)

            def first_gates():
                pe.wait_ge(s["h0_ready"], 1)
                pe.wait_ge(s["wh_split"], 3)
                pe.wait_ge(s["ring_read"], RING_LATE)
                for i in range(5):
                    seed(0, i)
                for m in range(EC):
                    for k in range(EC):
                        last = pe.matmul(pG[:, 0, m * B:(m + 1) * B], whT[:, k, m * P:(m + 1) * P],
                                         Hf[:, 2 * GS - 1, k * B:(k + 1) * B], start=False, stop=True,
                                         skip_group_check=True)
                last.then_inc(s["gate_sum"], 1)

            for i in range(FIRST):
                n, g = i // G, i % G
                scores(i)
                ring_items = ring_beside_unit(i)
                for j in range(4):
                    for r in ring_items[j * len(ring_items) // 4:(j + 1) * len(ring_items) // 4]:
                        ring(r)
                    if i:
                        values(i - 1, [j])
                if g == 2:
                    image_scores(n)
                if i == (HALF + 1) * G + 2:
                    for p in range(EC * G):
                        projection(0, p)

            first_gates()

            def step_gates(t):
                g, st = t // GS, t % GS
                prev = (t + 1) % 2
                for part, ready, weights in ((H1, "h_hi", (0, 1)), (H2, "h_low", (0,))):
                    pe.wait_ge(s[ready], t)
                    for m in range(EC):
                        dst = pG[:, g % 2, st * STEP + m * B:st * STEP + (m + 1) * B]
                        for w in weights:
                            for k in range(EC):
                                last = pe.matmul(dst, wh_parts[:, w, k, m * P:(m + 1) * P],
                                                 part[:, prev, k * B:(k + 1) * B], start=False, stop=True,
                                                 skip_group_check=True)
                last.then_inc(s["gate_sum"], 1)

            def rows_back(n, i):
                tb, b0 = n // (B // 2), 2 * (n % (B // 2))
                if i == 0:
                    pe.wait_ge(s["y_ready"], EC * (NG // TB) * (tb + 1))
                    if n >= 2:
                        pe.wait_ge(s["yt_copied"], n - 1)
                    else:
                        pe.wait_ge(s["prob_ready"], probs_done(UNITS - 1))
                ps = pS[:, n % 2, :]
                for k in range(EC):
                    last = pe.transpose(ps[:, i * E + k * P:i * E + (k + 1) * P], zT[:, k, tb, b0 + i, :], ident[:])
                if i:
                    last.then_inc(s["yt_full"], 1)

            for t in range(S):
                g, st = t // GS, t % GS
                if t:
                    step_gates(t)
                i, phase, last_phase, n, ug = at_step(t)
                if phase == 0 and i < UNITS:
                    scores(i)
                if phase in (1, 2) and i - 1 < UNITS:
                    values(i - 1, range(2 * phase - 2, 2 * phase))
                if last_phase and ug >= 2 and n < DUOS:
                    image_scores(n, range((ug - 2) * H // 2, (ug - 1) * H // 2))
                if t in PROJ_AT:
                    projection(*PROJ_AT[t])
                if t in RING_AT:
                    ring(RING_AT[t])
                if g + 1 < NG:
                    for p in SEED_AT.get(st, ()):
                        seed(g + 1, p)
                if 0 <= t - YT_FIRST < 4 * (B // 2) and (t - YT_FIRST) % 4 < 2:
                    rows_back((t - YT_FIRST) // 4, (t - YT_FIRST) % 4)
            for n in range(B // 2, DUOS // 2):
                for i in range(2):
                    rows_back(n, i)

        @block.scalar
        def _(act):
            for n, (kind, where, who) in enumerate(TILES):
                if who != "act":
                    continue
                act.wait_ge(s["tile_full"], n + 1)
                ps = bank(n)
                if kind == "x":
                    tb, k, hf = where
                    dst = xT[:, k, tb, hf * HALF:(hf + 1) * HALF, :].rearrange("p b q -> p (b q)")
                    act.activation(dst, ps, ACT.Copy).then_inc(s["act_tiles"], 1)
                elif kind == "cond":
                    act.activation(bias_cols[:], ps[:, STEP:STEP + 6 * EC], ACT.Copy).then_inc(s["bias_ready"], 1)
                    act.activation(Hf[:, 2 * GS - 1, :], ps[:, 0:STEP], ACT.Copy).then_inc(s["h0_ready"], 1)
                    act.activation(condT[:].rearrange("p k b -> p (k b)"), ps[:, 0:STEP], ACT.Copy
                                   ).then_inc(s["act_tiles"], 1)
                elif kind in ("uk", "wz"):
                    dst = {"uk": ukT, "wz": wzT[:]}[kind]
                    act.activation(dst.rearrange("p k e -> p (k e)"), ps, ACT.Copy,
                                   scale=2.0 if kind == "wz" else 1.0).then_inc(s["act_tiles"], 1)
                elif kind == "bg":
                    act.activation(b_gate_rows[:], ps[0:3 * EC, 0:P], ACT.Copy).then_inc(s["act_tiles"], 1)
                elif kind == "uv":
                    act.wait_ge(s["consts"], CONSTS)
                    act.activation(uvT.rearrange("p k (h c) -> p (k h) c", c=32)[:, :, 0:D],
                                   ps.rearrange("p (h d) -> p h d", d=D), ACT.Copy).then_inc(s["act_tiles"], 1)
                elif kind == "wh":
                    act.activation(whT[:].rearrange("p k e -> p (k e)"), ps, ACT.Copy).then_inc(s["wh_split"], 1)
                    act.activation(wh_parts[:, 0].rearrange("p k e -> p (k e)"), ps, ACT.Copy
                                   ).then_inc(s["act_tiles"], 1)
                elif kind in ("k", "q"):
                    tb, m, hf = where
                    i = SPLIT_OF[n]
                    c = m if kind == "q" else EC + m
                    scale = 0.25 if kind == "q" else 1.0
                    if i == 0:
                        act.wait_ge(s["b_scaled"], 2)
                    if i >= 2:
                        act.wait_ge(s["kq_mid"], i - 1)
                        act.wait_ge(s["kq_rest"], i - 1)
                        wait_stored(act, i - 2)
                    act.activation(full[:, i % 2], ps, ACT.Identity, bias=b_qk[:, c:c + 1], scale=scale
                                   ).then_inc(s["kq_hi"], 1)
                    act.activation(part_of(i, 0), ps if kind == "q" else ps.rearrange("p (b n) -> p b n", n=P),
                                   ACT.Identity, bias=b_qk[:, c:c + 1], scale=scale
                                   ).then_inc(s["kq_hi"], 1)
                    act.wait_ge(s["kq_hi"], 2 * (i + 1))
                    act.sem_inc(s["act_tiles"], 1)
                elif kind == "kimg":
                    for m in range(EC):
                        act.activation(img_full[:, m, :], ps[:, m * B:(m + 1) * B], ACT.Identity, bias=b_uk[:, m:m + 1]
                                       ).then_inc(s["img_hi"], 1)
                    for m in range(EC):
                        act.activation(parts_img[:, 0, m, :], ps[:, m * B:(m + 1) * B], ACT.Identity,
                                       bias=b_uk[:, m:m + 1]).then_inc(s["img_hi"], 1)
                    act.wait_ge(s["img_hi"], 2 * EC)
                    act.sem_inc(s["act_tiles"], 1)

            def weights(i, banks):
                qb = i // UNITS_0
                act.wait_ge(s["score_full"], i + 1)
                if i >= 2:
                    act.wait_ge(s["pv_full"], i - 1)
                for c in banks:
                    act.activation(prob[:, i % 2, c, :], pS[:, c if qb else i % 2, :], ACT.Exp
                                   ).then_inc(s["prob_ready"], 1)

            def image_weights(n):
                act.wait_ge(s["img_full_s"], n + 1)
                if n:
                    act.wait_ge(s["raw_ready"], G * n)
                act.activation(prob_img, pI[:], ACT.Exp).then_inc(s["img_prob"], 1)

            act.wait_ge(s["kq_mid"], len(SPLITS))
            act.wait_ge(s["kq_rest"], len(SPLITS))
            act.wait_ge(s["kq_low"], len(SPLITS))
            wait_stored(act, len(SPLITS) - 1)
            wait_stored(act, len(SPLITS) - 2)
            for i in range(FIRST):
                weights(i, range(i // UNITS_0 + 1))
                if i % G == 2:
                    image_weights(i // G)

            act.wait_ge(s["b_scaled"], 3)
            for t in range(S):
                g, st = t // GS, t % GS
                act.wait_ge(s["gate_sum"], t + 1)
                if t >= 2:
                    act.wait_ge(s["arg_ready"], t - 1)
                act.activation(gate[:, t % 2, :, 1], pG[:, g % 2, st * STEP:(st + 1) * STEP], ACT.Tanh,
                               scale=gate_scale[:, 0:1]).then_inc(s["gate_ready"], 1)
                act.wait_ge(s["arg_ready"], t + 1)
                if t >= 2:
                    act.wait_ge(s["h_low"], t - 1)
                act.activation(H1[:, t % 2], arg[:, t % 2, :, 1], ACT.Tanh).then_inc(s["h_hi"], 1)
                if st == 0:
                    if g >= 2:
                        act.wait_ge(s["y_ready"], EC * (g - 1))
                    else:
                        act.wait_ge(s["ones_q2"], 16)
                act.activation(Hf[:, t % (2 * GS), :], arg[:, t % 2, :, 1], ACT.Tanh).then_inc(s["h_full"], 1)
                i, phase, last_phase, n, ug = at_step(t)
                if i < UNITS and (phase == 1 or (phase == 2 and i >= UNITS_0)):
                    weights(i, [phase - 1])
                if phase == 0 and ug == 0 and FIRST // G < n <= DUOS:
                    image_weights(n - 1)
                if 0 <= t - YT_FIRST < 4 * (B // 2) and (t - YT_FIRST) % 4 == 2:
                    rows_out = (t - YT_FIRST) // 4
                    act.wait_ge(s["yt_full"], rows_out + 1)
                    if rows_out >= 2:
                        act.wait_ge(s[f"out_sent{rows_out % 2}"], 16 * (rows_out // 2))
                    act.activation(y_out[:, rows_out % 2].rearrange("p b e -> p (b e)"), pS[:, rows_out % 2, :],
                                   ACT.Copy).then_inc(s["yt_copied"], 1)

        @block.vector
        def _(dve):
            dve.wait_ge(s["bias_ready"], 1)
            dve.tensor_scalar(b_qk[:, 0:EC], b_qk[:, 0:EC], 0.25, None, ALU.mult).then_inc(s["b_scaled"], 1)
            dve.tensor_scalar(leak[:], alpha_in, -1.0, 1.0, ALU.mult, ALU.add).then_inc(s["b_scaled"], 1)
            dve.wait_ge(s["in_mask"], 16)
            dve.wait_ge(s["consts"], CONSTS)
            m_in, m_rest = [v.rearrange("b (t q) -> b t q", t=TB) for v in (mask_in, mask_rest)]
            m_part = [mask_parts[:, i, :, 1:KP] for i in range(3)]
            dve.tensor_copy(m_part[0], m_in).then_inc(s["mask_p"], 1)
            dve.wait_ge(s["mask_p"], 1)
            dve.tensor_tensor(m_rest, m_in, m_part[0], ALU.subtract).then_inc(s["mask_p"], 1)
            dve.wait_ge(s["mask_p"], 2)
            dve.tensor_copy(m_part[1], m_rest).then_inc(s["mask_p"], 1)
            dve.wait_ge(s["mask_p"], 3)
            dve.tensor_tensor(m_part[2], m_rest, m_part[1], ALU.subtract
                              ).then_inc(s["mask_p"], 1)

            def first_stage(n):
                kind, where, who = TILES[n]
                ps = bank(n)
                if kind in ("k", "q"):
                    i = SPLIT_OF[n]
                    dve.wait_ge(s["kq_hi"], 2 * (i + 1))
                    if i:
                        dve.wait_ge(s["kq_low"], i)
                    r = rest if kind == "q" else rest.rearrange("p (b n) -> p b n", n=P)
                    dve.tensor_tensor(r, full_of(i), part_of(i, 0), ALU.subtract
                                      ).then_inc(s["kq_rest"], 1)
                    dve.wait_ge(s["kq_mid"], i + 1)
                    dve.wait_ge(s["kq_rest"], i + 1)
                    dve.tensor_tensor(part_of(i, 2), r, part_of(i, 1), ALU.subtract
                                      ).then_inc(s["kq_low"], 1)
                elif kind == "kimg":
                    dve.wait_ge(s["img_hi"], 2 * EC)
                    dve.tensor_tensor(img_rest[:], img_full[:], parts_img[:, 0], ALU.subtract
                                      ).then_inc(s["img_rest_s"], 1)
                    dve.wait_ge(s["img_rest_s"], 1)
                    dve.tensor_copy(parts_img[:, 1], img_rest[:]).then_inc(s["img_mid"], 1)
                    dve.wait_ge(s["img_mid"], 1)
                    dve.tensor_tensor(parts_img[:, 2], img_rest[:], parts_img[:, 1], ALU.subtract
                                      ).then_inc(s["img_low"], 1)
                elif kind == "v":
                    tb, b0 = where
                    dve.wait_ge(s["tile_full"], n + 1)
                    dve.wait_ge(s["consts"], CONSTS)
                    for i in range(2):
                        ins = dve.tensor_tensor(V[:, tb, b0 + i, :, 0:D],
                                                ps[:, i * E:(i + 1) * E].rearrange("p (h d) -> p h d", h=H),
                                                b_v[:].rearrange("p (h d) -> p h d", h=H), ALU.add)
                    ins.then_inc(s["dve_tiles"], 1)
                elif kind == "vimg":
                    dve.wait_ge(s["tile_full"], n + 1)
                    dve.tensor_copy(Vimg[:].rearrange("p g b -> p (g b)"), ps[:, 0:G * B]
                                    ).then_inc(s["dve_tiles"], 1)
                elif kind == "wh":
                    dve.wait_ge(s["act_tiles"], tiles_done("act", n))
                    dve.wait_ge(s["wh_split"], 1)
                    w = [wh_parts[:, i].rearrange("p k e -> p (k e)") for i in range(2)]
                    dve.tensor_tensor(w[1], whT[:].rearrange("p k e -> p (k e)"), w[0], ALU.subtract
                                      ).then_inc(s["wh_split"], 2)

            def scale_rows():
                dve.wait_ge(s["in_rec"], 16)
                dve.tensor_reduce(tops[:], w_rec[:, :, 0:E], AX_X, ALU.max, apply_absolute_value=True
                                  ).then_inc(s["top_step"], 1)
                dve.wait_ge(s["top_step"], 1)
                dve.tensor_scalar(row_top[:], tops[:, 0:1], tops[:, 1:2], 2.0 ** -60, ALU.max, ALU.max
                                  ).then_inc(s["top_step"], 1)
                dve.wait_ge(s["top_step"], 2)
                bits = row_top[:].bitcast(I32)
                dve.tensor_scalar(bits, bits, 0x7F800000, None, ALU.bitwise_and).then_inc(s["top_step"], 1)
                dve.wait_ge(s["top_step"], 3)
                dve.tensor_scalar(row_top[:], row_top[:], 2.0 ** -14, None, ALU.mult).then_inc(s["top_step"], 1)
                dve.wait_ge(s["top_step"], 4)
                dve.reciprocal(row_scale[:], row_top[:]).then_inc(s["top_step"], 1)
                dve.tensor_scalar(gate_scale[:], row_top[:], 0.5, None, ALU.mult).then_inc(s["b_scaled"], 1)
                dve.wait_ge(s["top_step"], 5)
                for m in range(EC):
                    dve.tensor_scalar(w_rec[:, m], w_rec[:, m], row_scale[:, 0:1], None, ALU.mult
                                      ).then_inc(s["w_scaled"], 1)
                def step(ins, k):
                    ins.then_inc(s["b_step"], 1)
                    dve.wait_ge(s["b_step"], k)
                hi, parts, b_rest = b_gate_hi, b_gate_parts, b_gate_rest[:]
                step(dve.tensor_scalar(b_rest, b_gate, row_scale[:, 0:1], None, ALU.mult), 1)
                for i in range(3):
                    step(dve.tensor_copy(hi[:, i], b_rest), 3 * i + 2)
                    step(dve.tensor_copy(parts[:, i], hi[:, i]), 3 * i + 3)
                    step(dve.tensor_tensor(b_rest, b_rest, hi[:, i], ALU.subtract), 3 * i + 4)
                dve.sem_inc(s["w_scaled"], 1)

            def ring(n):
                kind, w = RING[n][:2]
                dve.wait_ge(s["ring_full"], n + 1)
                if kind == "max":
                    _, _, duo, h0, nh = RING[n]
                    cols = 1 + P * (w // 2) + keys_seen(w)
                    dve.tensor_reduce(row_max[:, w % 2].rearrange("p (h b) -> p h b", b=HALF)[:, h0:h0 + nh, duo],
                                      ring_bank(n)[:, 0:nh * cols].rearrange("p (h c) -> p h c", h=nh), AX_X, ALU.max
                                      ).then_inc(s["ring_read"], 1)
                    return
                k = 5 * w
                if w:
                    dve.wait_ge(s["shift_sent"], 48 * w)
                dve.tensor_scalar(shift[:], ring_bank(n)[0:H * HALF, 0:P], -1.0, None, ALU.mult
                                  ).then_inc(s["ring_read"], 1)
                dve.wait_ge(s["ring_read"], n + 1)
                dve.tensor_copy(shift_parts[:, 0], shift[:]).then_inc(s["shift_step"], 2)
                dve.wait_ge(s["shift_step"], k + 2)
                dve.tensor_tensor(shift_rest[:], shift[:], shift_parts[:, 0], ALU.subtract
                                  ).then_inc(s["shift_step"], 1)
                dve.wait_ge(s["shift_step"], k + 3)
                dve.tensor_copy(shift_parts[:, 1], shift_rest[:]).then_inc(s["shift_step"], 1)
                dve.wait_ge(s["shift_step"], k + 4)
                dve.tensor_tensor(shift_parts[:, 2], shift_rest[:], shift_parts[:, 1], ALU.subtract
                                  ).then_inc(s["shift_step"], 1)

            def add_image(n, g):
                if g == 0:
                    dve.wait_ge(s["pv_full"], G * (n + 1))
                    dve.wait_ge(s["img_prob"], n + 1)
                    if n >= 2:
                        dve.wait_ge(s["att_ready"], G * (n - 1))
                for e in range(2):
                    b, c = 2 * (n % HALF) + e, slice(g * P + e * QT, g * P + (e + 1) * QT)
                    last = dve.scalar_tensor_tensor(att_raw[n % 2][:, c], prob_img[:, c], Vimg[:, g, b:b + 1],
                                                    pV[:, c], ALU.mult, ALU.add)
                last.then_inc(s["raw_ready"], 1)

            def invert(n):
                dve.wait_ge(s["den_sent"], 16 * (n + 1))
                if n:
                    dve.wait_ge(s["inv_stored"], 16 * n)
                dve.reciprocal(den_inv[:], den[:]).then_inc(s["den_inverted"], 1)

            def divide(n, g):
                w = n // HALF
                if g == 0:
                    dve.wait_ge(s["inv_spread"], 64 * (n + 1))
                    if w >= 2:
                        dve.wait_ge(s["proj_full"], EC * (w - 1))
                c = slice(g * P, (g + 1) * P)
                dve.tensor_tensor(att[:, w % 2, g, n % HALF, :], att_raw[n % 2][:, c], att_inv[:, c], ALU.mult
                                  ).then_inc(s["att_ready"], 1)

            def add_x(w, m, i):
                dve.wait_ge(s["proj_full"], EC * w + m + 1)
                ps = projection_bank(w, m)
                z = zT[:, m, w // 2, i * HALF:(i + 1) * HALF, (w % 2) * QT:(w % 2 + 1) * QT]
                p = ps[:, i * HALF * QT:(i + 1) * HALF * QT].rearrange("p (b q) -> p b q", b=HALF)
                dve.scalar_tensor_tensor(z, p, b_proj[:, m:m + 1], z, ALU.add, ALU.add).then_inc(s["z_ready"], 1)

            for n in range(len(TILES_A)):
                first_stage(n)
            dve.wait_ge(s["stack_k0"], 96)
            dve.wait_ge(s["stack_k1"], 96)
            dve.wait_ge(s["mask_stacked"], 16 * TB)
            dve.wait_ge(s["ones_k"], 16)
            dve.wait_ge(s["img_stacked"], 96)
            dve.tensor_copy(Kst[0:ROWS, 0].rearrange("p h (b n) -> p h b n", n=KP)[:, :, :, 0], Kimg[0:ROWS]
                            ).then_inc(s["img_placed"], 1)
            for n in range(len(TILES_B)):
                if n == 6:
                    scale_rows()
                for r in ring_beside_tile(n):
                    ring(r)
                first_stage(len(TILES_A) + n)
            wait_stored(dve, len(SPLITS) - 1)
            wait_stored(dve, len(SPLITS) - 2)
            for i in range(FIRST):
                n, g = i // G, i % G
                for r in ring_beside_unit(i):
                    ring(r)
                if g == 0 and n:
                    for c in range(G):
                        add_image(n - 1, c)
                if g == 2 and n:
                    invert(n - 1)
                if g == 1 and n >= 2:
                    for c in range(G):
                        divide(n - 2, c)
                if i == (HALF + 1) * G + 2:
                    for m in range(EC):
                        for c in range(2):
                            add_x(0, m, c)

            def attention_piece(t, side):
                i, phase, last_phase, n, ug = at_step(t)
                if t - 1 in RING_AT and side == 0:
                    ring(RING_AT[t - 1])
                k = t - starts(G * n) - 3
                if 0 <= k < 2 and n - 1 < DUOS:
                    add_image(n - 1, 2 * k + side)
                if t in DIVIDE_AT:
                    divide(DIVIDE_AT[t][0], 2 * DIVIDE_AT[t][1] + side)
                if t == inverted_at(n - 1) and side == 0 and n - 1 < DUOS:
                    invert(n - 1)
                if (t, side) in Z_AT:
                    add_x(*Z_AT[t, side])

            dve.wait_ge(s["h0_ready"], 1)
            for t in range(S):
                g, st = t // GS, t % GS
                prev = (t + 2 * GS - 1) % (2 * GS)
                pair = zq[:, g % 2, st]
                if t:
                    dve.wait_ge(s["h_full"], t)
                    if t >= 2:
                        dve.wait_ge(s["gate_sum"], t)
                    dve.tensor_tensor(H2[:, (t - 1) % 2], Hf[:, prev, :], H1[:, (t - 1) % 2], ALU.subtract
                                      ).then_inc(s["h_low"], 1)
                if st == 0:
                    dve.wait_ge(s["zq_ready"], EC * (g + 1))
                for k in range(EC):
                    c = slice(k * B, (k + 1) * B)
                    dve.scalar_tensor_tensor(pair[:, c, 1], Hf[:, prev, c], leak[:, k:k + 1], pair[:, c, 0],
                                             ALU.mult, ALU.add).then_inc(s["q_ready"], 1)
                attention_piece(t, 0)
                dve.wait_ge(s["gate_ready"], t + 1)
                dve.wait_ge(s["q_ready"], EC * (t + 1))
                dve.tensor_tensor_scan(arg[:, t % 2].rearrange("p a b -> p (a b)"),
                                       gate[:, t % 2].rearrange("p a b -> p (a b)"),
                                       pair.rearrange("p a b -> p (a b)"), 0.0, ALU.mult, ALU.add
                                       ).then_inc(s["arg_ready"], 1)
                attention_piece(t, 1)

            for n in range(B // 2, DUOS // 2):
                dve.wait_ge(s["yt_full"], n + 1)
                dve.wait_ge(s[f"out_sent{n % 2}"], 16 * (n // 2))
                dve.tensor_copy(y_out[:, n % 2].rearrange("p b e -> p (b e)"), pS[:, n % 2, :]
                                ).then_inc(s["yt_copied"], 1)


_INS = ["x", "cond_1024", "mask_Bx1x1xS_ff0", "L0_cond_c_attn_w", "L0_cond_c_attn_b", "L0_cond_c_proj_w",
        "L0_cond_c_proj_b", "L0_cond_uk_w", "L0_cond_uk_b", "L0_cond_uv_w", "L0_cond_uv_b", "L1_cond_W",
        "L1_cond_b", "L1_cond_alpha"]


def kernel(**inputs):
    import numpy as np
    import concourse.bacc as bacc
    from concourse.bass_utils import run_bass_kernel_spmd as run

    nc = bacc.Bacc("TRN2", target_bir_lowering=False, num_devices=1)
    arrays, args = {}, []
    for name in _INS:
        a = np.ascontiguousarray(inputs[name])
        arrays[f"in_{name}"] = a
        args.append(nc.dram_tensor(f"in_{name}", a.shape, mybir.dt.from_np(a.dtype), kind="ExternalInput").ap())
    out = nc.dram_tensor("out_0", (8, 256, 256), F32, kind="ExternalOutput").ap()
    build(nc, *args, out)
    r = run(nc, [arrays], core_ids=[0])
    return r.results[0]["out_0"]
```
